# Optimizing a Trainium2 kernel written in Bass

```python
import numpy as np
import jax
import jax.numpy as jnp

def _softmax(x, axis=-1):
    return jax.nn.softmax(x, axis=axis)

def _gelu(x):
    return jax.nn.gelu(x, approximate=True)

def _silu(x):
    return jax.nn.silu(x)

def _sigmoid(x):
    return jax.nn.sigmoid(x)

def _layernorm(x, axis=-1, eps=1e-05):
    m = jnp.mean(x, axis=axis, keepdims=True)
    v = jnp.var(x, axis=axis, keepdims=True)
    return (x - m) / jnp.sqrt(v + eps)

def _scatter_add(tgt, idx, src, axis=0):
    return tgt.at[idx].add(src)

def _segment_sum(src, seg, n):
    return jax.ops.segment_sum(src, seg, n)
kernel_name = 'mk_cond_resid_d2_seqx_r2_30b40a'

def setup_inputs(seed: int=0):
    np.random.seed(seed)
    _w = jnp.asarray

    def _rec_inputs():
        import jax
        import jax.numpy as jnp
        _rk = jax.random.key(seed)
        x = -0.0002928 + 1 * jax.random.normal(jax.random.fold_in(_rk, 1), (8, 512, 512), jnp.float32)
        _lenS = 512 - jax.random.randint(jax.random.fold_in(_rk, 7), (8,), 0, max(1, 512 // 4) + 1, jnp.int32)
        _lenS2 = 512 - jax.random.randint(jax.random.fold_in(_rk, 8), (8,), 0, max(1, 512 // 4) + 1, jnp.int32)
        fside_16xSxS_0 = -5.72187e-05 + 0.999849 * jax.random.normal(jax.random.fold_in(_rk, 11), (16, 512, 512), jnp.float32)
        cond_64 = -0.0265395 + 0.99382 * jax.random.normal(jax.random.fold_in(_rk, 13), (8, 64), jnp.float32)
        _validS = jnp.arange(512)[None, :] < _lenS[:, None]
        _validS2 = jnp.arange(512)[None, :] < _lenS2[:, None]
        _causal = jnp.tril(jnp.ones((512, 512), dtype=bool))
        mask_BxS_bk0 = jnp.logical_not(jnp.broadcast_to(_validS[:, :], (8, 512)))
        return (x, fside_16xSxS_0, cond_64, mask_BxS_bk0)
    x, fside_16xSxS_0, cond_64, mask_BxS_bk0 = _rec_inputs()

    def _L0_cond_setup():
        import jax, jax.numpy as jnp
        import numpy as np
        B, N, DIM, H, DH = (2, 1024, 512, 16, 64)
        INNER = H * DH
        EPS = 1e-05

        def layernorm(x, g):
            mean = jnp.mean(x, axis=-1, keepdims=True)
            var = jnp.var(x, axis=-1, keepdims=True)
            return (x - mean) * jax.lax.rsqrt(var + EPS) * g
        key = jax.random.key(seed)
        ks = jax.random.split(key, 10)
        x = jax.random.normal(ks[0], (B, N, DIM), dtype=jnp.float32)
        attn_bias = jax.random.normal(ks[1], (H, N, N), dtype=jnp.float32)
        mask = jax.random.randint(ks[2], (B, N), 0, 2).astype(bool)
        g_in = jnp.ones((DIM,), dtype=jnp.float32)
        null_attn_bias = jax.random.normal(ks[3], (H,), dtype=jnp.float32)
        null_kv = jax.random.normal(ks[4], (2, DH), dtype=jnp.float32)
        Wq = jax.random.normal(ks[5], (DIM, INNER), dtype=jnp.float32) * 0.02
        Wkv = jax.random.normal(ks[6], (DIM, 2 * DH), dtype=jnp.float32) * 0.02
        Wo = jax.random.normal(ks[7], (INNER, DIM), dtype=jnp.float32) * 0.02
        g_out = jnp.ones((DIM,), dtype=jnp.float32)
        return {'x': x, 'attn_bias': attn_bias, 'mask': mask, 'g_in': g_in, 'null_attn_bias': null_attn_bias, 'null_kv': null_kv, 'Wq': Wq, 'Wkv': Wkv, 'Wo': Wo, 'g_out': g_out}
    _L0_cond_all = _L0_cond_setup()
    _L0_cond_in = {k: v for k, v in _L0_cond_all.items() if k in ('g_in', 'null_attn_bias', 'Wq', 'Wkv', 'Wo', 'g_out')}
    del _L0_cond_all

    def _L1_cond_setup():
        import jax, jax.numpy as jnp
        import numpy as np
        B, S, H = (4, 1024, 512)
        E = 8
        M = 256
        K = 2
        N_SHARED = 2
        SM = M * N_SHARED
        G = 64
        GE_TEMP = 1.0
        ALPHA = 0.001
        SEQ_AUX = True
        NORM_TOPK = True
        COS_TEMP = 0.78
        CONS_ALPHA = 0.01
        LEAKY_SLOPE = 0.01
        EPS_COS = 1e-08

        def _leaky(x):
            return jnp.where(x >= 0, x, LEAKY_SLOPE * x)

        def _moe_forward(hidden_states, g, wt, wg, w_gate, w_up, w_down, sw_gate, sw_up, sw_down):
            b, s, h = hidden_states.shape
            x = hidden_states.reshape(-1, h)
            T = x.shape[0]
            logits_h = x @ wt.T
            logits_g = g @ wg.T
            logits_g = jnp.repeat(logits_g, s, axis=0)
            logits = (logits_h + logits_g / GE_TEMP) / (1.0 + 1.0 / GE_TEMP)
            scores = jax.nn.softmax(logits, axis=-1)
            topk_w, topk_idx = jax.lax.top_k(scores, K)
            if K > 1 and NORM_TOPK:
                topk_w = topk_w / (topk_w.sum(-1, keepdims=True) + 1e-20)
            onehot = jax.nn.one_hot(topk_idx.reshape(b, s * K), E, dtype=jnp.float32)
            ce = onehot.sum(1) / (s * K / E)
            aux_loss = (ce * scores.reshape(b, s, E).mean(1)).sum(1).mean() * ALPHA
            gp = _leaky(jnp.einsum('th,ehm->etm', x, w_gate))
            up = jnp.einsum('th,ehm->etm', x, w_up)
            y_all = jnp.einsum('etm,emh->eth', gp * up, w_down)
            y_sel = y_all[topk_idx, jnp.arange(T)[:, None], :]
            y = (y_sel * topk_w[..., None]).sum(1).reshape(b, s, h)
            p = _leaky(hidden_states @ sw_gate) * (hidden_states @ sw_up) @ sw_down
            y = y + p
            num = jnp.sum(y * p, -1)
            den = jnp.maximum(jnp.linalg.norm(y, axis=-1), EPS_COS) * jnp.maximum(jnp.linalg.norm(p, axis=-1), EPS_COS)
            closs = CONS_ALPHA * jnp.mean(num / den / (1.0 + COS_TEMP))
            return (y, aux_loss + closs)
        key = jax.random.key(seed)
        ks = jax.random.split(key, 12)
        sh = 1.0 / np.sqrt(H)
        sm = 1.0 / np.sqrt(M)
        ssm = 1.0 / np.sqrt(SM)
        sg = 1.0 / np.sqrt(G)
        return {'hidden_states': jax.random.normal(ks[0], (B, S, H), jnp.float32), 'g': jax.random.normal(ks[1], (B, G), jnp.float32), 'wt': jax.random.uniform(ks[2], (E, H), jnp.float32, -sh, sh), 'wg': jax.random.uniform(ks[3], (E, G), jnp.float32, -sg, sg), 'w_gate': jax.random.uniform(ks[4], (E, H, M), jnp.float32, -sh, sh), 'w_up': jax.random.uniform(ks[5], (E, H, M), jnp.float32, -sh, sh), 'w_down': jax.random.uniform(ks[6], (E, M, H), jnp.float32, -sm, sm), 'sw_gate': jax.random.uniform(ks[7], (H, SM), jnp.float32, -sh, sh), 'sw_up': jax.random.uniform(ks[8], (H, SM), jnp.float32, -sh, sh), 'sw_down': jax.random.uniform(ks[9], (SM, H), jnp.float32, -ssm, ssm)}
    _L1_cond_all = _L1_cond_setup()
    _L1_cond_in = {k: v for k, v in _L1_cond_all.items() if k in ('wt', 'wg', 'w_gate', 'w_up', 'w_down', 'sw_gate', 'sw_up', 'sw_down')}
    del _L1_cond_all
    return {'x': x, 'fside_16xSxS_0': fside_16xSxS_0, 'cond_64': cond_64, 'mask_BxS_bk0': mask_BxS_bk0, 'L0_cond_g_in': _L0_cond_in['g_in'], 'L0_cond_null_attn_bias': _L0_cond_in['null_attn_bias'], 'L0_cond_Wq': _L0_cond_in['Wq'], 'L0_cond_Wkv': _L0_cond_in['Wkv'], 'L0_cond_Wo': _L0_cond_in['Wo'], 'L0_cond_g_out': _L0_cond_in['g_out'], 'L1_cond_wt': _L1_cond_in['wt'], 'L1_cond_wg': _L1_cond_in['wg'], 'L1_cond_w_gate': _L1_cond_in['w_gate'], 'L1_cond_w_up': _L1_cond_in['w_up'], 'L1_cond_w_down': _L1_cond_in['w_down'], 'L1_cond_sw_gate': _L1_cond_in['sw_gate'], 'L1_cond_sw_up': _L1_cond_in['sw_up'], 'L1_cond_sw_down': _L1_cond_in['sw_down']}

def reference(x, fside_16xSxS_0, cond_64, mask_BxS_bk0, L0_cond_g_in, L0_cond_null_attn_bias, L0_cond_Wq, L0_cond_Wkv, L0_cond_Wo, L0_cond_g_out, L1_cond_wt, L1_cond_wg, L1_cond_w_gate, L1_cond_w_up, L1_cond_w_down, L1_cond_sw_gate, L1_cond_sw_up, L1_cond_sw_down):
    import jax
    import jax.numpy as jnp

    def _L0_cond_ref(x, attn_bias, mask, g_in, null_attn_bias, null_kv, Wq, Wkv, Wo, g_out):
        import jax, jax.numpy as jnp
        import numpy as np
        B, N, DIM, H, DH = (2, 1024, 512, 16, 64)
        INNER = H * DH
        EPS = 1e-05

        def layernorm(x, g):
            mean = jnp.mean(x, axis=-1, keepdims=True)
            var = jnp.var(x, axis=-1, keepdims=True)
            return (x - mean) * jax.lax.rsqrt(var + EPS) * g
        b, n, _ = x.shape
        scale = DH ** (-0.5)
        xn = layernorm(x, g_in)
        q = (xn @ Wq).reshape(b, n, H, DH).transpose(0, 2, 1, 3) * scale
        kv = xn @ Wkv
        k, v = (kv[..., :DH], kv[..., DH:])
        nk = jnp.broadcast_to(null_kv[0], (b, 1, DH))
        nv = jnp.broadcast_to(null_kv[1], (b, 1, DH))
        k = jnp.concatenate([nk, k], axis=1)
        v = jnp.concatenate([nv, v], axis=1)
        sim = jnp.einsum('bhid,bjd->bhij', q, k)
        null_col = jnp.broadcast_to(null_attn_bias[:, None, None], (H, n, 1))
        bias = jnp.concatenate([null_col, attn_bias], axis=-1)
        sim = sim + bias
        neg = -jnp.finfo(sim.dtype).max
        j = n + 1
        causal_mask = jnp.triu(jnp.ones((n, j), dtype=bool), k=j - n + 1)
        sim = jnp.where(causal_mask, neg, sim)
        mask_p = jnp.pad(mask, ((0, 0), (1, 0)), constant_values=True)
        sim = jnp.where(mask_p[:, None, None, :], sim, neg)
        attn = jax.nn.softmax(sim, axis=-1)
        out = jnp.einsum('bhij,bjd->bhid', attn, v)
        out = out.transpose(0, 2, 1, 3).reshape(b, n, INNER)
        out = out @ Wo
        return layernorm(out, g_out)

    def _L1_cond_ref(hidden_states, g, wt, wg, w_gate, w_up, w_down, sw_gate, sw_up, sw_down):
        import jax, jax.numpy as jnp
        import numpy as np
        B, S, H = (4, 1024, 512)
        E = 8
        M = 256
        K = 2
        N_SHARED = 2
        SM = M * N_SHARED
        G = 64
        GE_TEMP = 1.0
        ALPHA = 0.001
        SEQ_AUX = True
        NORM_TOPK = True
        COS_TEMP = 0.78
        CONS_ALPHA = 0.01
        LEAKY_SLOPE = 0.01
        EPS_COS = 1e-08

        def _leaky(x):
            return jnp.where(x >= 0, x, LEAKY_SLOPE * x)

        def _moe_forward(hidden_states, g, wt, wg, w_gate, w_up, w_down, sw_gate, sw_up, sw_down):
            b, s, h = hidden_states.shape
            x = hidden_states.reshape(-1, h)
            T = x.shape[0]
            logits_h = x @ wt.T
            logits_g = g @ wg.T
            logits_g = jnp.repeat(logits_g, s, axis=0)
            logits = (logits_h + logits_g / GE_TEMP) / (1.0 + 1.0 / GE_TEMP)
            scores = jax.nn.softmax(logits, axis=-1)
            topk_w, topk_idx = jax.lax.top_k(scores, K)
            if K > 1 and NORM_TOPK:
                topk_w = topk_w / (topk_w.sum(-1, keepdims=True) + 1e-20)
            onehot = jax.nn.one_hot(topk_idx.reshape(b, s * K), E, dtype=jnp.float32)
            ce = onehot.sum(1) / (s * K / E)
            aux_loss = (ce * scores.reshape(b, s, E).mean(1)).sum(1).mean() * ALPHA
            gp = _leaky(jnp.einsum('th,ehm->etm', x, w_gate))
            up = jnp.einsum('th,ehm->etm', x, w_up)
            y_all = jnp.einsum('etm,emh->eth', gp * up, w_down)
            y_sel = y_all[topk_idx, jnp.arange(T)[:, None], :]
            y = (y_sel * topk_w[..., None]).sum(1).reshape(b, s, h)
            p = _leaky(hidden_states @ sw_gate) * (hidden_states @ sw_up) @ sw_down
            y = y + p
            num = jnp.sum(y * p, -1)
            den = jnp.maximum(jnp.linalg.norm(y, axis=-1), EPS_COS) * jnp.maximum(jnp.linalg.norm(p, axis=-1), EPS_COS)
            closs = CONS_ALPHA * jnp.mean(num / den / (1.0 + COS_TEMP))
            return (y, aux_loss + closs)
        y, _ = _moe_forward(hidden_states, g, wt, wg, w_gate, w_up, w_down, sw_gate, sw_up, sw_down)
        return y
    x = x + _L0_cond_ref(x, fside_16xSxS_0, mask_BxS_bk0, L0_cond_g_in, L0_cond_null_attn_bias, cond_64, L0_cond_Wq, L0_cond_Wkv, L0_cond_Wo, L0_cond_g_out)
    x = x + _L1_cond_ref(x, cond_64, L1_cond_wt, L1_cond_wg, L1_cond_w_gate, L1_cond_w_up, L1_cond_w_down, L1_cond_sw_gate, L1_cond_sw_up, L1_cond_sw_down)
    return x

_drawn_inputs = setup_inputs


def setup_inputs(seed=0):
    import zlib

    import numpy as np

    out = dict(_drawn_inputs(seed))
    spreads = {'L0_cond_g_in': (1.0, 0.2), 'L0_cond_g_out': (1.0, 0.2)}
    factors = {}
    for name, (base, spread) in spreads.items():
        noise = np.random.default_rng([zlib.crc32(name.encode()), seed]).standard_normal(out[name].shape)
        drawn = base * np.exp(spread * noise) if base else spread * noise
        out[name] = jnp.asarray(drawn.astype(out[name].dtype))
    for name, factor in factors.items():
        out[name] = (out[name] * factor).astype(out[name].dtype)
    return out
```

```python
import concourse.bass as bass
from concourse import mybir
from contextlib import ExitStack

F32 = mybir.dt.float32
F32R = mybir.dt.float32r
I32 = mybir.dt.int32
U8 = mybir.dt.uint8
U32 = mybir.dt.uint32
ALU = mybir.AluOpType
ACT = mybir.ActivationFunctionType
AX = mybir.AxisListType

P = 128
B, S, D = 8, 512, 512
H, DH = 16, 64
INNER = H * DH
TB = S // P
T = B * TB
DC = D // P
IC = INNER // P
E, M, TOPK = 8, 256, 2
SM = 2 * M
SC = SM // P
MC = M // P
G = 64
SLOT_TILES = T * TOPK + E
EPS = 1e-5
TINY = 1e-20
LEAK = 0.01
MASKED = 2.0 ** 120
BANK = 512
HALF = H // 2
AHEAD = 2
CK = [AHEAD + P * (i + 1) for i in range(TB)]
BIAS_AT = [H * sum(CK[:i]) for i in range(TB)]
EW = DC * 2 * M + MC * D


def build(nc, x, fside, cond, mask, g_in, null_bias, Wq, Wkv, Wo, g_out,
          wt, wg, w_gate, w_up, w_down, sw_gate, sw_up, sw_down, out):
    dram = {
        "q_hi": nc.dram_tensor("q_hi_d", (B, INNER, S), F32, kind="Internal").ap(),
        "q_lo": nc.dram_tensor("q_lo_d", (B, INNER, S), F32, kind="Internal").ap(),
        "k_hi": nc.dram_tensor("k_hi_d", (B, DH, S), F32, kind="Internal").ap(),
        "k_lo": nc.dram_tensor("k_lo_d", (B, DH, S), F32, kind="Internal").ap(),
        "mask": nc.dram_tensor("mask_d", (1, B * S), F32, kind="Internal").ap(),
        "o": nc.dram_tensor("o_d", (B * S, INNER), F32, kind="Internal").ap(),
        "x1": nc.dram_tensor("x1_d", (B * S, D), F32, kind="Internal").ap(),
        "ys": nc.dram_tensor("ys_d", (SLOT_TILES * P, D), F32, kind="Internal").ap(),
    }
    with ExitStack() as ctx:
        psum = ctx.enter_context(nc.psum_tensor("psum", [P, 8 * BANK], F32))
        resident = ctx.enter_context(nc.sbuf_tensor("resident", [P, E * EW], F32))
        ident = ctx.enter_context(nc.sbuf_tensor("ident", [P, P], F32))
        pow_half = ctx.enter_context(nc.sbuf_tensor("pow_half", [P, TB], F32))
        eps = ctx.enter_context(nc.sbuf_tensor("eps", [P, TB], F32))
        constants_set = ctx.enter_context(nc.semaphore("constants_set"))
        stage_constants(nc, ident, pow_half, eps, constants_set)
        spare = {eng: ctx.enter_context(nc.sbuf_tensor(f"spare_{eng}", [1, TB], F32)) for eng in ("dve", "pool")}
        with ExitStack() as held:
            values = held.enter_context(nc.sbuf_tensor("values", [P, B, TB, DH], F32))
            stage_project(nc, x, fside, cond, mask, g_in, null_bias, Wq, Wkv, dram, psum, resident, ident,
                          pow_half, eps, spare, values)
            stage_attend(nc, cond, dram, psum, resident, ident, spare, values)
        with ExitStack() as held:
            logits = held.enter_context(nc.sbuf_tensor("logits", [P, T, E], F32))
            route = {
                "weights": held.enter_context(nc.sbuf_tensor("top_weights", [P, TOPK, T], F32)),
                "slots": held.enter_context(nc.sbuf_tensor("slots", [P, TOPK, T], I32)),
                "tokens": held.enter_context(nc.sbuf_tensor("slot_tokens", [P, SLOT_TILES], I32)),
                "experts": held.enter_context(nc.sbuf_tensor("tile_experts", [1, SLOT_TILES], I32)),
            }
            experts_loaded = held.enter_context(nc.semaphore("experts_loaded"))
            stage_output(nc, x, cond, Wo, g_out, wt, wg, w_gate, w_up, w_down, dram, psum, resident, ident,
                         pow_half, eps, spare, logits, experts_loaded)
            shared = {half: [held.enter_context(nc.sbuf_tensor(f"shared_{half}{n}", [P, DC, SM], F32R)) for n in range(3)]
                      for half in ("hi", "lo")}
            stage_route(nc, sw_gate, sw_up, sw_down, psum, logits, shared, route)
            stage_experts(nc, dram, psum, resident, ident, spare, route)
            stage_shared(nc, dram, psum, resident, ident, spare, shared, route, out)


def bank(psum, i):
    return psum[:, i * BANK:(i + 1) * BANK]


def bias_of(resident, i, h):
    at = BIAS_AT[i] + h * CK[i]
    return resident[:, at:at + CK[i]]


def stage_constants(nc, ident, pow_half, eps, constants_set):
    with nc.Block() as block:
        @block.gpsimd
        def _(pool):
            pool.memset(ident[:], 0.0).then_inc(constants_set, 1)
            pool.memset(pow_half[:], -0.5).then_inc(constants_set, 1)
            pool.memset(eps[:], EPS).then_inc(constants_set, 1)
            pool.wait_ge(constants_set, 3)
            pool.affine_select(out=ident[:], in_=ident[:], compare_op=ALU.not_equal, fill=1.0, base=0,
                               pattern=[[-1, P]], channel_multiplier=1).then_inc(constants_set, 1)


def stage_project(nc, x, fside, cond, mask, g_in, null_bias, Wq, Wkv, dram, psum, resident, ident, pow_half,
                  eps, spare, values):
    with ExitStack() as ctx:
        def sb(name, shape, dt=F32):
            return ctx.enter_context(nc.sbuf_tensor(name, shape, dt))

        def sem(name):
            return ctx.enter_context(nc.semaphore(name))

        wq_hi, wq_lo = sb("wq_hi", [P, DC, INNER], F32R), sb("wq_lo", [P, DC, INNER], F32R)
        wkv_hi, wkv_lo = sb("wkv_hi", [P, DC, 2 * DH], F32R), sb("wkv_lo", [P, DC, 2 * DH], F32R)
        g_col = sb("g_col", [P, DC])
        xin = sb("xin", [P, TB, D])
        stats, moments, rstd = sb("stats", [P, TB, 6]), sb("moments", [P, TB, 2]), sb("rstd", [P, TB])
        xT_hi = [sb(f"xT_hi{i}", [P, DC, S], F32R) for i in range(2)]
        xT_lo = [sb(f"xT_lo{i}", [P, DC, S], F32R) for i in range(2)]
        q_hi, q_lo = sb("q_hi", [P, 2, S], F32R), sb("q_lo", [P, 2, S], F32R)
        k_hi, k_lo = sb("k_hi", [DH, S], F32R), sb("k_lo", [DH, S], F32R)
        kv_out = sb("kv_out", [P, S])
        wq_rest = sb("wq_rest", [P, DC, INNER // 2])
        null_bias_sb = sb("null_bias_sb", [P, H])
        at = BIAS_AT[-1] + H * CK[-1]
        wq_stage = [resident[:, at:at + INNER * DC // 2].rearrange("p (c n) -> p c n", c=DC),
                    wq_rest[:]]
        at += INNER * DC // 2
        wkv_stage = resident[:, at:at + DC * 2 * DH].rearrange("p (c n) -> p c n", c=DC)
        at += DC * 2 * DH
        mask_row = resident[0:1, at:at + B * S // 4].bitcast(U8)
        mask_out = xT_hi[1][0:1, :, :].rearrange("p c s -> p (c s)")

        loaded = sem("small_inputs_loaded")
        wq_loaded, wkv_loaded = sem("wq_loaded"), sem("wkv_loaded")
        bias_loaded = [sem(f"bias_loaded{i}") for i in range(TB)]
        bias_ready = sem("bias_ready")
        weights_hi, weights_lo = sem("weights_hi"), sem("weights_lo")
        x_loaded = sem("x_loaded")
        ln_stats, ln_moments, ln_shifted, ln_rstd = sem("ln_stats"), sem("ln_moments"), sem("ln_shifted"), sem("ln_rstd")
        xn_ready = sem("xn_ready")
        xT_full, xT_hi_ready, xT_lo_ready = sem("xT_full"), sem("xT_hi_ready"), sem("xT_lo_ready")
        proj_full, q_hi_ready, q_lo_ready = sem("proj_full"), sem("q_hi_ready"), sem("q_lo_ready")
        q_stored = [sem(f"q_stored{k}") for k in range(2)]
        k_lo_ready, k_stored, mask_stored = sem("k_lo_ready"), sem("k_stored"), sem("mask_stored")
        kv_copied, vT_full, v_copied = sem("kv_copied"), sem("vT_full"), sem("v_copied")
        mask_ready = sem("mask_ready")

        NP = IC + 1
        x_bank = [bank(psum, 0), bank(psum, 1)]
        proj_bank = [bank(psum, 2 + k) for k in range(4)]
        v_bank = bank(psum, 6)
        SMALL = 16 * 3

        block = ctx.enter_context(nc.Block())

        @block.sync
        def _(sp):
            def load_x(b):
                sp.dma_start(xin[:], x[bass.ds(b, 1)].rearrange("a (t p) d -> p (a t) d", p=P)).then_inc(x_loaded, 16)

            def store_q(b):
                for n in range(IC):
                    sp.wait_ge(q_lo_ready, IC * b + n + 1)
                    for name, half in (("q_hi", q_hi), ("q_lo", q_lo)):
                        sp.dma_start(dram[name][bass.ds(b, 1), n * P:(n + 1) * P, :].rearrange("a p s -> p (a s)"),
                                     half[:, n % 2, :].bitcast(F32)).then_inc(q_stored[n % 2], 16)
                sp.wait_ge(k_lo_ready, b + 1)
                for name, half in (("k_hi", k_hi), ("k_lo", k_lo)):
                    sp.dma_start(dram[name][bass.ds(b, 1)].rearrange("a p s -> p (a s)"), half[:].bitcast(F32)
                                 ).then_inc(k_stored, 16)

            load_x(0)
            for j in range(2):
                sp.dma_start(wq_stage[j], Wq[:, j * INNER // 2:(j + 1) * INNER // 2].rearrange("(c p) n -> p c n", p=P)
                             ).then_inc(wq_loaded, 16)
            sp.dma_start(wkv_stage, Wkv.rearrange("(c p) n -> p c n", p=P)).then_inc(wkv_loaded, 16)
            sp.wait_ge(xT_full, DC)
            load_x(1)
            with sp.Fori(0, B - 2) as b:
                sp.wait_ge(xT_full, DC * b + 2 * DC)
                load_x(b + 2)
                store_q(b)
            store_q(B - 2)
            store_q(B - 1)
            for k in range(2):
                sp.wait_ge(q_stored[k], 16 * IC * B)
            sp.wait_ge(k_stored, 16 * 2 * B)
            sp.wait_ge(mask_stored, 16 * 2)

        @block.gpsimd
        def _(pool):
            pool.dma_start(g_col[:], g_in.rearrange("(c p) -> p c", p=P), allow_slow_non_contiguous=True
                           ).then_inc(loaded, 16)
            pool.dma_start(mask_row, mask.rearrange("(a b) s -> a (b s)", a=1)).then_inc(loaded, 16)
            pool.dma_start(null_bias_sb[:], null_bias.partition_broadcast(P)).then_inc(loaded, 16)

            def reciprocal_std(b):
                pool.wait_ge(ln_moments, TB * b + TB)
                pool.tensor_tensor(out=rstd[:], in0=moments[:, :, 1], in1=eps[:], op=ALU.add).then_inc(ln_shifted, 1)
                pool.wait_ge(ln_shifted, b + 1)
                pool.tensor_tensor(out=rstd[:], in0=rstd[:], in1=pow_half[:], op=ALU.pow).then_inc(ln_rstd, 1)

            def negate_biases(i):
                at = BIAS_AT[i]
                tile = resident[:, at:at + H * CK[i]].rearrange("p (h n) -> p h n", h=H)
                pool.wait_ge(bias_loaded[i], 16)
                pool.tensor_scalar(out=tile[:, :, AHEAD:CK[i]], in0=tile[:, :, AHEAD:CK[i]], scalar1=-1.0, scalar2=1.0,
                                   op0=ALU.mult, op1=ALU.mult).then_inc(bias_ready, 1)
                pool.tensor_scalar(out=tile[:, :, 0], in0=null_bias_sb[:], scalar1=-1.0, scalar2=1.0,
                                   op0=ALU.mult, op1=ALU.mult).then_inc(bias_ready, 1)
                pool.memset(tile[:, :, 1], MASKED).then_inc(bias_ready, 1)
                pool.wait_ge(bias_ready, 4 * i + 3)
                last = tile[:, :, CK[i] - P:CK[i]]
                pool.affine_select(out=last, in_=last, compare_op=ALU.is_ge, fill=MASKED, base=0,
                                   pattern=[[0, H], [-1, P]], channel_multiplier=1).then_inc(bias_ready, 1)

            reciprocal_std(0)
            pool.wait_ge(loaded, SMALL)
            reciprocal_std(1)
            for i in range(TB):
                negate_biases(i)
                reciprocal_std(2 + i)
            for b in range(2 + TB, B):
                reciprocal_std(b)

        @block.vector
        def _(dve):
            def normalise(b):
                dve.wait_ge(x_loaded, 16 * b + 16)
                for t in range(TB):
                    dve.bn_stats(stats[:, t, :], xin[:, t, :]).then_inc(ln_stats, 1)
                for t in range(TB):
                    dve.wait_ge(ln_stats, TB * b + t + 1)
                    dve.memset(spare["dve"][:, t:t + 1], 0.0)
                    dve.bn_aggr(moments[:, t, :], stats[:, t, :]).then_inc(ln_moments, 1)
                dve.wait_ge(ln_moments, TB * b + TB)
                dve.wait_ge(ln_rstd, b + 1)
                for t in range(TB):
                    dve.tensor_scalar(out=xin[:, t, :], in0=xin[:, t, :], scalar1=moments[:, t, 0:1],
                                      scalar2=rstd[:, t:t + 1], op0=ALU.subtract, op1=ALU.mult).then_inc(xn_ready, 1)

            def split_low(b, k):
                for c in range(DC):
                    dve.wait_ge(xT_hi_ready, DC * b + c + 1)
                    dve.scalar_tensor_tensor(out=xT_lo[k][:, c, :], in0=x_bank[c % 2], scalar=g_col[:, c:c + 1],
                                             in1=xT_hi[k][:, c, :].bitcast(F32), op0=ALU.mult, op1=ALU.subtract
                                             ).then_inc(xT_lo_ready, 1)

            def lower_q(b, ns):
                for n in ns:
                    dve.wait_ge(q_hi_ready, IC * b + n + 1)
                    dve.scalar_tensor_tensor(out=q_lo[:, n % 2, :], in0=proj_bank[n % 4], scalar=-float(DH) ** -0.5,
                                             in1=q_hi[:, n % 2, :].bitcast(F32), op0=ALU.mult, op1=ALU.subtract
                                             ).then_inc(q_lo_ready, 1)

            def lower_k(b):
                dve.wait_ge(kv_copied, 2 * b + 2)
                dve.tensor_tensor(out=k_lo[:], in0=kv_out[0:DH, :], in1=k_hi[:].bitcast(F32), op=ALU.subtract
                                  ).then_inc(k_lo_ready, 1)

            def copy_v(b):
                dve.wait_ge(vT_full, b + 1)
                dve.tensor_copy(values[:, bass.ds(b, 1), :, :].rearrange("p a t d -> p (a t) d"),
                                v_bank.rearrange("p (t n) -> p t n", t=TB)[:, :, DH:2 * DH]).then_inc(v_copied, 1)

            def step(b, k, before=True, split=True, norm=True):
                if split:
                    split_low(b + 1, 1 - k)
                if before:
                    copy_v(b - 1)
                lower_q(b, range(0, IC // 2))
                if norm:
                    normalise(b + 2)
                lower_q(b, range(IC // 2, IC))
                lower_k(b)

            normalise(0)
            dve.wait_ge(loaded, SMALL)
            for j in range(2):
                dve.wait_ge(mask_stored, 16 * j)
                dve.tensor_scalar(out=mask_out, in0=mask_row[:, j * B * S // 2:(j + 1) * B * S // 2],
                                  scalar1=-MASKED, scalar2=MASKED, op0=ALU.mult, op1=ALU.add).then_inc(mask_ready, 1)
            dve.wait_ge(weights_hi, 3)
            dve.tensor_tensor(out=wkv_lo[:], in0=wkv_stage, in1=wkv_hi[:].bitcast(F32), op=ALU.subtract
                              ).then_inc(weights_lo, 1)
            for j in range(2):
                part = slice(j * INNER // 2, (j + 1) * INNER // 2)
                dve.tensor_tensor(out=wq_lo[:, :, part], in0=wq_stage[j], in1=wq_hi[:, :, part].bitcast(F32),
                                  op=ALU.subtract).then_inc(weights_lo, 1)
            split_low(0, 0)
            normalise(1)
            step(0, 0, before=False)
            with dve.Fori(0, (B - 4) // 2) as g:
                step(2 * g + 1, 1)
                step(2 * g + 2, 0)
            step(B - 3, 1)
            step(B - 2, 0, norm=False)
            step(B - 1, 1, split=False, norm=False)
            copy_v(B - 1)

        @block.scalar
        def _(act):
            def split_high(b, k):
                if not (isinstance(b, int) and b == 0):
                    act.wait_ge(proj_full, NP * b - NP)
                for c in range(DC):
                    act.wait_ge(xT_full, DC * b + c + 1)
                    act.activation(xT_hi[k][:, c, :], x_bank[c % 2], ACT.Copy, scale=g_col[:, c:c + 1]
                                   ).then_inc(xT_hi_ready, 1)

            def copy_q(b):
                for n in range(IC):
                    act.wait_ge(proj_full, NP * b + n + 1)
                    act.wait_ge(q_stored[n % 2], 32 * (IC // 2 * b + n // 2))
                    act.activation(q_hi[:, n % 2, :], proj_bank[n % 4], ACT.Copy, scale=-float(DH) ** -0.5
                                   ).then_inc(q_hi_ready, 1)
                act.wait_ge(proj_full, NP * b + NP)
                act.wait_ge(vT_full, b)
                act.wait_ge(k_lo_ready, b)
                act.activation(kv_out[:], proj_bank[IC % 4], ACT.Copy).then_inc(kv_copied, 1)
                act.wait_ge(k_stored, 32 * b)
                act.activation(k_hi[:], proj_bank[IC % 4][0:DH, :], ACT.Copy).then_inc(kv_copied, 1)

            for i in range(TB):
                at = BIAS_AT[i]
                tile = resident[:, at:at + H * CK[i]].rearrange("p (h n) -> p h n", h=H)
                act.dma_start(tile[:, :, AHEAD:CK[i]], fside[:, i * P:(i + 1) * P, 0:CK[i] - AHEAD].rearrange("h p n -> p h n")
                              ).then_inc(bias_loaded[i], 16)
            act.wait_ge(wkv_loaded, 16)
            act.activation(wkv_hi[:], wkv_stage, ACT.Copy).then_inc(weights_hi, 1)
            act.wait_ge(wq_loaded, 32)
            for j in range(2):
                act.activation(wq_hi[:, :, j * INNER // 2:(j + 1) * INNER // 2], wq_stage[j], ACT.Copy
                               ).then_inc(weights_hi, 1)
            act.wait_ge(loaded, SMALL)
            for j in range(2):
                act.wait_ge(mask_ready, j + 1)
                act.dma_start(dram["mask"][:, j * B * S // 2:(j + 1) * B * S // 2], mask_out.bitcast(F32)
                              ).then_inc(mask_stored, 16)
            act.wait_ge(mask_stored, 32)
            split_high(0, 0)
            split_high(1, 1)
            copy_q(0)
            with act.Fori(0, (B - 2) // 2) as g:
                split_high(2 * g + 2, 0)
                copy_q(2 * g + 1)
                split_high(2 * g + 3, 1)
                copy_q(2 * g + 2)
            copy_q(B - 1)

        @block.tensor
        def _(pe):
            def transpose_x(b):
                pe.wait_ge(xn_ready, TB * b + TB)
                for c in range(DC):
                    if not (isinstance(b, int) and b == 0 and c < 2):
                        pe.wait_ge(xT_lo_ready, DC * b + c - 1)
                    for t in range(TB):
                        last = pe.transpose(x_bank[c % 2][:, t * P:(t + 1) * P], xin[:, t, c * P:(c + 1) * P], ident[:])
                    last.then_inc(xT_full, 1)

            def transpose_v(b):
                pe.wait_ge(kv_copied, 2 * b + 2)
                pe.wait_ge(v_copied, b)
                for t in range(TB):
                    last = pe.transpose(v_bank[:, t * P:(t + 1) * P], kv_out[:, t * P:(t + 1) * P], ident[:])
                last.then_inc(vT_full, 1)

            def project(b, k):
                pe.wait_ge(xT_lo_ready, DC * b + DC)
                for n in range(NP):
                    if n == 0:
                        pe.wait_ge(kv_copied, 2 * b)
                    elif n < 4:
                        pe.wait_ge(q_lo_ready, IC * b)
                    else:
                        pe.wait_ge(q_lo_ready, IC * b + n - 3)
                    if n < IC:
                        hi, lo = wq_hi[:, :, n * P:(n + 1) * P], wq_lo[:, :, n * P:(n + 1) * P]
                    else:
                        hi, lo = wkv_hi[:], wkv_lo[:]
                    out = proj_bank[n % 4]
                    for c in range(DC):
                        pe.matmul(out, hi[:, c, :], xT_hi[k][:, c, :], start=(c == 0), stop=False)
                        pe.matmul(out, hi[:, c, :], xT_lo[k][:, c, :], start=False, stop=False)
                        last = pe.matmul(out, lo[:, c, :], xT_hi[k][:, c, :], start=False, stop=(c == DC - 1))
                    last.then_inc(proj_full, 1)

            transpose_x(0)
            transpose_x(1)
            pe.wait_ge(weights_lo, 3)
            project(0, 0)
            with pe.Fori(0, (B - 2) // 2) as g:
                for i in range(2):
                    b = 2 * g + 1 + i
                    transpose_x(b + 1)
                    transpose_v(b - 1)
                    project(b, 1 - i)
            transpose_v(B - 2)
            project(B - 1, 1)
            transpose_v(B - 1)


def stage_attend(nc, cond, dram, psum, resident, ident, spare, values):
    with ExitStack() as ctx:
        def sb(name, shape, dt=F32):
            return ctx.enter_context(nc.sbuf_tensor(name, shape, dt))

        def sem(name):
            return ctx.enter_context(nc.semaphore(name))

        queries = [sb(f"queries{i}", [P, H, P], F32R) for i in range(2)]
        queries1 = [sb(f"queries_and_ones{i}", [P, H, P], F32R) for i in range(2)]
        keys = sb("keys", [P, 2, AHEAD + S], F32R)
        keys1 = sb("keys_lo_and_mask", [P, 2, AHEAD + S], F32R)
        scores = [sb(f"scores{i}", [P, AHEAD + S]) for i in range(2)]
        null_key = sb("null_key", [P, 1])
        lowest = sb("lowest", [P, 4])
        probs = [sb(f"probs{i}", [P, HALF, AHEAD + S]) for i in range(2)]
        probsT = [sb(f"probsT{i}", [P, S]) for i in range(2)]
        sums, rsums = sb("sums", [P, 2, HALF]), sb("rsums", [P, 2, HALF])
        null_weight, null_out = sb("null_weight", [P, HALF]), sb("null_out", [P, HALF, DH])
        null_value = sb("null_value", [P, DH])
        o_out = [sb(f"o_out{i}", [P, HALF, DH]) for i in range(2)]

        queries_loaded = [sem(f"queries_loaded{i}") for i in range(2)]
        keys_loaded = sem("keys_loaded")
        null_loaded, null_split = sem("null_loaded"), sem("null_split")
        ones_set, keys_cleared = sem("ones_set"), sem("keys_cleared")
        scores_full, scores_biased = sem("scores_full"), sem("scores_biased")
        probs_ready, probsT_full = sem("probs_ready"), sem("probsT_full")
        probsT_even, probsT_odd = sem("probsT_even"), sem("probsT_odd")
        heads_summed, rsums_ready = sem("heads_summed"), sem("rsums_ready")
        o_scaled = [sem(f"o_scaled{i}") for i in range(2)]
        null_weighted = [sem(f"null_weighted{i}") for i in range(2)]
        null_spread, o_ready = sem("null_spread"), sem("o_ready")
        o_stored = [sem(f"o_stored{i}") for i in range(2)]

        CUT = AHEAD + 2 * P
        UB = TB * H
        HB = UB // HALF
        PASSES = [(queries, keys[:].rearrange("p b n -> p (b n)")), (queries1, keys1[:].rearrange("p b n -> p (b n)"))]

        def score_psum(i, u):
            start = 2 * BANK * (u % 2) + (BANK - CUT if CK[i] > BANK else 0)
            return psum[:, start:start + CK[i]]

        probsT_bank = [bank(psum, 4), bank(psum, 5)]
        o_bank = [bank(psum, 6), bank(psum, 7)]

        block = ctx.enter_context(nc.Block())

        @block.sync
        def _(sp):
            def load_queries(b, i):
                for dst, name in ((queries[i % 2][0:DH], "q_hi"), (queries[i % 2][DH:P], "q_lo"),
                                  (queries1[i % 2][0:DH], "q_hi")):
                    sp.dma_start(dst.bitcast(F32), dram[name][bass.ds(b, 1), :, i * P:(i + 1) * P].rearrange(
                        "a (h d) p -> d (a h) p", d=DH)).then_inc(queries_loaded[i % 2], 16)

            def load_keys(b):
                for dst, name in ((keys[0:DH], "k_hi"), (keys[DH:P], "k_hi"), (keys1[0:DH], "k_lo")):
                    sp.dma_start(dst[:, bass.ds(b % 2, 1), AHEAD:AHEAD + S].rearrange("p a s -> p (a s)").bitcast(F32), dram[name][bass.ds(b, 1)].rearrange("a p s -> p (a s)")
                                 ).then_inc(keys_loaded, 16)
                sp.dma_start(keys1[DH:DH + 1, bass.ds(b % 2, 1), AHEAD:AHEAD + S].rearrange("p a s -> p (a s)").bitcast(F32),
                             dram["mask"][:, bass.ds(b * S, S)]
                             ).then_inc(keys_loaded, 16)

            def body(b, last):
                for k in range(HB):
                    if k % 2 == 0 and (k < TB or not last):
                        sp.wait_ge(scores_full, UB * b + H * (k // 2 + 1))
                        if k < TB:
                            load_queries(b, 2 + k // 2)
                        else:
                            if k == TB:
                                load_keys(b + 1)
                            load_queries(b + 1, k // 2 - 2)
                    sp.wait_ge(o_ready, HB * b + k + 1)
                    sp.dma_start(dram["o"][bass.ds(b * S + k // 2 * P, P), k % 2 * HALF * DH:(k % 2 + 1) * HALF * DH],
                                 o_out[k % 2][:].rearrange("p h d -> p (h d)")).then_inc(o_stored[k % 2], 16)

            sp.dma_start(null_value[:], cond[1:2, :].rearrange("a d -> (a d)").partition_broadcast(P)
                         ).then_inc(null_loaded, 16)
            for part in (slice(0, DH), slice(DH, P)):
                sp.dma_start(null_key[part, :], cond[0:1, :].rearrange("a d -> d a"), allow_slow_non_contiguous=True
                             ).then_inc(null_loaded, 16)
            sp.wait_ge(keys_cleared, 3)
            load_keys(0)
            load_queries(0, 0)
            load_queries(0, 1)
            with sp.Fori(0, B - 1) as b:
                body(b, False)
            body(B - 1, True)
            for k in range(2):
                sp.wait_ge(o_stored[k], 16 * B * HB // 2)

        @block.gpsimd
        def _(pool):
            pool.wait_ge(null_loaded, 48)
            with pool.Fori(0, B) as b:
                for k in range(HB):
                    pool.wait_ge(o_scaled[k % 2], HB // 2 * b + k // 2 + 1)
                    pool.tensor_tensor(out=null_weight[:], in0=probs[k % 2][:, :, 0], in1=rsums[:, k % 2, :],
                                       op=ALU.mult).then_inc(null_weighted[k % 2], 1)
                    pool.wait_ge(null_weighted[k % 2], HB // 2 * b + k // 2 + 1)
                    pool.tensor_tensor(out=null_out[:], in0=null_weight[:].unsqueeze(2).to_broadcast([P, HALF, DH]),
                                       in1=null_value[:].unsqueeze(1).to_broadcast([P, HALF, DH]),
                                       op=ALU.mult).then_inc(null_spread, 1)
                    pool.wait_ge(null_spread, HB * b + k + 1)
                    pool.tensor_tensor(out=o_out[k % 2][:], in0=o_out[k % 2][:], in1=null_out[:],
                                       op=ALU.add).then_inc(o_ready, 1)
                    pool.wait_ge(o_ready, HB * b + k + 1)

        @block.vector
        def _(dve):
            def add_bias(b, n):
                i, h = n // H, n % H
                dve.wait_ge(scores_full, UB * b + n + 1)
                if not (isinstance(b, int) and b == 0 and n == 0):
                    dve.wait_ge(probs_ready, UB * b + n - 1)
                dve.memset(spare["dve"][:, n % 2:n % 2 + 1], 0.0)
                dve.tensor_tensor_reduce(out=scores[n % 2][:, 0:CK[i]], in0=score_psum(i, n), in1=bias_of(resident, i, h),
                                         scale=1.0, scalar=3.0e38, op0=ALU.add, op1=ALU.min,
                                         accum_out=lowest[:, n % 4:n % 4 + 1]).then_inc(scores_biased, 1)

            def copy_probs(b, n):
                dve.wait_ge(probsT_full, UB * b + n + 1)
                dve.tensor_copy(probsT[n % 2][:, 0:CK[n // H] - AHEAD], probsT_bank[n % 2][:, 0:CK[n // H] - AHEAD]
                                ).then_inc(probsT_odd, 1)

            def scale_half(b, k):
                dve.wait_ge(heads_summed, HB * b + k + 1)
                dve.reciprocal(rsums[:, k % 2, :], sums[:, k % 2, :]).then_inc(rsums_ready, 1)
                dve.wait_ge(rsums_ready, HB * b + k + 1)
                dve.wait_ge(o_stored[k % 2], 16 * (HB // 2 * b + k // 2))
                dve.tensor_tensor(out=o_out[k % 2][:], in0=o_bank[k % 2].rearrange("p (h d) -> p h d", d=DH),
                                  in1=rsums[:, k % 2, :].unsqueeze(2).to_broadcast([P, HALF, DH]),
                                  op=ALU.mult).then_inc(o_scaled[k % 2], 1)

            def body(b, last):
                for n in range(UB):
                    if n + 1 < UB:
                        add_bias(b, n + 1)
                    elif not last:
                        add_bias(b + 1, 0)
                    if n % 2:
                        copy_probs(b, n)
                    if n % HALF == 1 and n > HALF:
                        scale_half(b, n // HALF - 1)
                scale_half(b, HB - 1)

            dve.memset(keys[:, :, 0:AHEAD].bitcast(F32), 0.0).then_inc(keys_cleared, 1)
            dve.memset(keys1[0:DH, :, 0:AHEAD].bitcast(F32), 0.0).then_inc(keys_cleared, 1)
            dve.memset(keys1[DH:P, :, :].bitcast(F32), 0.0).then_inc(keys_cleared, 1)
            for i in range(2):
                dve.memset(queries1[i][DH:P, :, :].bitcast(F32), 1.0).then_inc(ones_set, 1)
            dve.wait_ge(null_loaded, 48)
            dve.wait_ge(keys_cleared, 2)
            dve.tensor_copy(keys[:, :, 0], null_key[:].to_broadcast([P, 2])).then_inc(null_split, 1)
            dve.wait_ge(null_split, 1)
            dve.tensor_tensor(out=keys1[0:DH, :, 0], in0=null_key[0:DH, :].to_broadcast([DH, 2]),
                              in1=keys[0:DH, :, 0].bitcast(F32), op=ALU.subtract).then_inc(null_split, 1)
            add_bias(0, 0)
            with dve.Fori(0, B - 1) as b:
                body(b, False)
            body(B - 1, True)

        @block.scalar
        def _(act):
            def exponential(b, n):
                i, h, k = n // H, n % H, n // HALF
                act.wait_ge(scores_biased, UB * b + n + 1)
                if h % HALF == 0:
                    act.wait_ge(null_weighted[k % 2], HB // 2 * b + k // 2)
                act.activation(probs[k % 2][:, h % HALF, 0:CK[i]], scores[n % 2][:, 0:CK[i]], ACT.Exp,
                               bias=lowest[:, n % 4:n % 4 + 1], scale=-1.0,
                               accum_out=sums[:, k % 2, h % HALF:h % HALF + 1]).then_inc(probs_ready, 1)

            def copy_probs(b, n):
                act.wait_ge(probsT_full, UB * b + n + 1)
                act.activation(probsT[n % 2][:, 0:CK[n // H] - AHEAD], probsT_bank[n % 2][:, 0:CK[n // H] - AHEAD], ACT.Copy
                               ).then_inc(probsT_even, 1)

            def body(b, last):
                for n in range(UB):
                    if n + 1 < UB:
                        exponential(b, n + 1)
                    elif not last:
                        exponential(b + 1, 0)
                    if n % 2 == 0:
                        copy_probs(b, n)

            exponential(0, 0)
            with act.Fori(0, B - 1) as b:
                body(b, False)
            body(B - 1, True)

        @block.tensor
        def _(pe):
            def score(b, n):
                i, h = n // H, n % H
                if n == 0:
                    pe.wait_ge(keys_loaded, 64 * b + 64)
                if h == 0:
                    pe.wait_ge(queries_loaded[i % 2], 48 * (2 * b + i // 2 + 1))
                if not (isinstance(b, int) and b == 0 and n < 2):
                    pe.wait_ge(scores_biased, UB * b + n - 1)
                whole = score_psum(i, n)
                parts = [(0, CUT), (CUT, CK[i])] if CK[i] > BANK else [(0, CK[i])]
                for lo, hi in parts:
                    for p, (qs, ks) in enumerate(PASSES):
                        last = pe.matmul(whole[:, lo:hi], qs[i % 2][:, h, :],
                                         ks[:, bass.ds((b % 2) * (AHEAD + S) + lo, hi - lo)], start=(p == 0), stop=(p == 1))
                last.then_inc(scores_full, 1)

            def transpose_probs(b, n):
                i, h, k = n // H, n % H, n // HALF
                pe.wait_ge(probs_ready, UB * b + n + 1)
                pe.wait_ge(probsT_odd if n % 2 else probsT_even, UB // 2 * b + n // 2)
                for j in range(i + 1):
                    last = pe.transpose(probsT_bank[n % 2][:, j * P:(j + 1) * P],
                                        probs[k % 2][:, h % HALF, AHEAD + j * P:AHEAD + (j + 1) * P], ident[:])
                last.then_inc(probsT_full, 1)

            def weigh_values(b, n):
                i, h, k = n // H, n % H, n // HALF
                pe.wait_ge(probsT_odd if n % 2 else probsT_even, UB // 2 * b + n // 2 + 1)
                if h % HALF == 0:
                    pe.wait_ge(o_scaled[k % 2], HB // 2 * b + k // 2)
                for j in range(i + 1):
                    last = pe.matmul(o_bank[k % 2][:, h % HALF * DH:(h % HALF + 1) * DH],
                                     probsT[n % 2][:, j * P:(j + 1) * P],
                                     values[:, bass.ds(b, 1), j, :].rearrange("p a d -> p (a d)"),
                                     start=(j == 0), stop=(j == i))
                if h % HALF == HALF - 1:
                    last.then_inc(heads_summed, 1)

            def body(b, last):
                for n in range(UB):
                    if n + 2 < UB:
                        score(b, n + 2)
                    elif not last:
                        score(b + 1, n + 2 - UB)
                    transpose_probs(b, n)
                    if n:
                        weigh_values(b, n - 1)
                weigh_values(b, UB - 1)

            pe.wait_ge(ones_set, 2)
            pe.wait_ge(null_split, 2)
            score(0, 0)
            score(0, 1)
            with pe.Fori(0, B - 1) as b:
                body(b, False)
            body(B - 1, True)



def stage_output(nc, x, cond, Wo, g_out, wt, wg, w_gate, w_up, w_down, dram, psum, resident, ident, pow_half,
                 eps, spare, logits, experts_loaded):
    with ExitStack() as ctx:
        def sb(name, shape, dt=F32):
            return ctx.enter_context(nc.sbuf_tensor(name, shape, dt))

        def sem(name):
            return ctx.enter_context(nc.semaphore(name))

        wo_stage = sb("wo_stage", [P, IC, D])
        wo_hi, wo_lo = sb("wo_hi", [P, IC, D], F32R), sb("wo_lo", [P, IC, D], F32R)
        g_rows = sb("g_rows", [P, D])
        wt_T, wg_T, cond_T = sb("wt_T", [P, DC, E]), sb("wg_T", [G, E]), sb("cond_T", [G, B])
        group = sb("group_logits", [P, B, E])
        o_in = [sb(f"o_in{i}", [P, INNER]) for i in range(2)]
        x_in = [sb(f"x_in{i}", [P, D]) for i in range(2)]
        oT_hi = [sb(f"oT_hi{i}", [P, IC, P], F32R) for i in range(2)]
        oT_lo = [sb(f"oT_lo{i}", [P, IC, P], F32R) for i in range(2)]
        stats, moments, rstd = sb("stats3", [P, 6]), sb("moments3", [P, 2, 2]), sb("rstd3", [P, 2])
        x1 = [sb(f"x1_{i}", [P, D]) for i in range(2)]
        x1T = sb("x1T", [P, DC, P])

        wo_loaded, small_loaded = sem("wo_loaded"), sem("small3_loaded")
        wo_hi_ready, wo_lo_ready = sem("wo_hi_ready"), sem("wo_lo_ready")
        group_full, group_copied = sem("group_full"), sem("group_copied")
        o_loaded = [sem(f"o_loaded{i}") for i in range(2)]
        x_loaded = [sem(f"x_rows_loaded{i}") for i in range(2)]
        oT_full, oT_hi_ready, oT_lo_ready = sem("oT_full"), sem("oT_hi_ready"), sem("oT_lo_ready")
        out_full = sem("out_full")
        ln_stats, ln_moments, ln_shifted, ln_rstd = (sem("ln3_stats"), sem("ln3_moments"), sem("ln3_shifted"),
                                                     sem("ln3_rstd"))
        y_ready, y_scaled, x1_ready = sem("y_ready"), sem("y_scaled"), sem("x1_ready")
        x1_stored = [sem(f"x1_stored{i}") for i in range(2)]
        x1T_full, x1T_copied, logits_full, logits_copied = (sem("x1T_full"), sem("x1T_copied"), sem("logits_full"),
                                                            sem("logits_copied"))

        x_rows = x.rearrange("b s d -> (b s) d")
        oT_bank = [[bank(psum, 2 * k + j) for j in range(2)] for k in range(2)]
        out_bank = [bank(psum, 4 + k) for k in range(2)]
        x1T_bank, logits_bank = bank(psum, 6), bank(psum, 7)

        def steps(eng, step):
            for t in range(2):
                step(t, t % 2, t // 2)
            with eng.Fori(1, T // 2 - 1) as m:
                for k in range(2):
                    step(2 * m + k, k, m)
            for t in range(T - 2, T):
                step(t, t % 2, t // 2)

        def known(t):
            return isinstance(t, int)

        block = ctx.enter_context(nc.Block())

        @block.sync
        def _(sp):
            def load_o(t, k):
                sp.dma_start(o_in[k][:], dram["o"][bass.ds(t * P, P), :]).then_inc(o_loaded[k], 16)

            def load_x(t, k):
                sp.dma_start(x_in[k][:], x_rows[bass.ds(t * P, P), :]).then_inc(x_loaded[k], 16)

            def store_x1(t, k):
                sp.wait_ge(x1_ready, t + 1)
                sp.dma_start(dram["x1"][bass.ds(t * P, P), :], x1[k][:]).then_inc(x1_stored[k], 16)

            def step(t, k, m):
                if not (known(t) and t + 2 >= T):
                    sp.wait_ge(oT_full, 2 * t + 2)
                    load_o(t + 2, k)
                if not (known(t) and t == 0):
                    store_x1(t - 1, 1 - k)
                if not (known(t) and t + 1 >= T):
                    load_x(t + 1, 1 - k)

            load_o(0, 0)
            sp.dma_start(wo_stage[:], Wo.rearrange("(c p) n -> p c n", p=P)).then_inc(wo_loaded, 16)
            load_o(1, 1)
            load_x(0, 0)
            steps(sp, step)
            store_x1(T - 1, 1)
            for k in range(2):
                sp.wait_ge(x1_stored[k], 16 * T // 2)

        @block.gpsimd
        def _(pool):
            pool.dma_start(g_rows[:], g_out.partition_broadcast(P)).then_inc(small_loaded, 16)
            with nc.allow_non_contiguous_dma(reason="small weights, transposed as they come"):
                pool.dma_start(wg_T[:], wg.rearrange("e g -> g e")).then_inc(small_loaded, 16)
                pool.dma_start(cond_T[:], cond.rearrange("b g -> g b")).then_inc(small_loaded, 16)
                for c in range(DC):
                    pool.dma_start(wt_T[:, c, :], wt[:, c * P:(c + 1) * P].rearrange("e p -> p e")
                                   ).then_inc(small_loaded, 16)
            pool.wait_ge(small_loaded, 16 * (3 + DC))

            def step(t, k, m):
                pool.wait_ge(ln_moments, t + 1)
                pool.tensor_tensor(out=rstd[:, k:k + 1], in0=moments[:, k, 1:2], in1=eps[:, 0:1], op=ALU.add
                                   ).then_inc(ln_shifted, 1)
                pool.wait_ge(ln_shifted, t + 1)
                pool.tensor_tensor(out=rstd[:, k:k + 1], in0=rstd[:, k:k + 1], in1=pow_half[:, 0:1], op=ALU.pow
                                   ).then_inc(ln_rstd, 1)
                pool.wait_ge(y_ready, t + 1)
                pool.tensor_tensor(out=x1[k][:], in0=x1[k][:], in1=g_rows[:], op=ALU.mult).then_inc(y_scaled, 1)
                pool.wait_ge(y_scaled, t + 1)
                pool.wait_ge(x_loaded[k], 16 * m + 16)
                pool.tensor_tensor(out=x1[k][:], in0=x1[k][:], in1=x_in[k][:], op=ALU.add).then_inc(x1_ready, 1)

            steps(pool, step)

        @block.vector
        def _(dve):
            def split_low(t, k):
                for j in range(2):
                    dve.wait_ge(oT_hi_ready, 2 * t + j + 1)
                    dve.tensor_tensor(out=oT_lo[k][:, 4 * j:4 * j + 4, :].rearrange("p c n -> p (c n)"), in0=oT_bank[k][j],
                                      in1=oT_hi[k][:, 4 * j:4 * j + 4, :].rearrange("p c n -> p (c n)").bitcast(F32),
                                      op=ALU.subtract).then_inc(oT_lo_ready, 1)

            def step(t, k, m):
                if not (known(t) and t + 1 >= T):
                    split_low(t + 1, 1 - k)
                dve.wait_ge(out_full, t + 1)
                dve.bn_stats(stats[:], out_bank[k]).then_inc(ln_stats, 1)
                dve.wait_ge(ln_stats, t + 1)
                dve.memset(spare["dve"][:, 0:1], 0.0)
                dve.bn_aggr(moments[:, k, :], stats[:]).then_inc(ln_moments, 1)
                dve.wait_ge(ln_moments, t + 1)
                dve.wait_ge(ln_rstd, t + 1)
                dve.wait_ge(x1_stored[k], 16 * m)
                if not (known(t) and t < 2):
                    dve.wait_ge(x1T_full, t - 1)
                dve.tensor_scalar(out=x1[k][:], in0=out_bank[k], scalar1=moments[:, k, 0:1], scalar2=rstd[:, k:k + 1],
                                  op0=ALU.subtract, op1=ALU.mult).then_inc(y_ready, 1)

            dve.wait_ge(wo_hi_ready, 1)
            dve.tensor_tensor(out=wo_lo[:], in0=wo_stage[:], in1=wo_hi[:].bitcast(F32), op=ALU.subtract
                              ).then_inc(wo_lo_ready, 1)
            dve.wait_ge(group_full, 1)
            dve.tensor_copy(group[:], x1T_bank[:, 0:B * E].rearrange("p (b e) -> p b e", e=E)).then_inc(group_copied, 1)
            split_low(0, 0)
            steps(dve, step)
            dve.wait_ge(logits_full, T)
            dve.wait_ge(group_copied, 1)
            dve.tensor_tensor(out=logits[:].rearrange("p (b t) e -> p b t e", t=TB),
                              in0=logits_bank[:, 0:T * E].rearrange("p (b t e) -> p b t e", t=TB, e=E),
                              in1=group[:].unsqueeze(2).to_broadcast([P, B, TB, E]), op=ALU.add
                              ).then_inc(logits_copied, 1)

        @block.scalar
        def _(act):
            def split_high(t, k):
                if not (known(t) and t < 2):
                    act.wait_ge(out_full, t - 1)
                for j in range(2):
                    act.wait_ge(oT_full, 2 * t + j + 1)
                    act.activation(oT_hi[k][:, 4 * j:4 * j + 4, :].rearrange("p c n -> p (c n)"), oT_bank[k][j], ACT.Copy
                                   ).then_inc(oT_hi_ready, 1)

            def copy_x1T(t):
                act.wait_ge(x1T_full, t + 1)
                act.activation(x1T[:].rearrange("p c n -> p (c n)"), x1T_bank, ACT.Copy).then_inc(x1T_copied, 1)

            def step(t, k, m):
                if not (known(t) and t + 1 >= T):
                    split_high(t + 1, 1 - k)
                if not (known(t) and t == 0):
                    copy_x1T(t - 1)

            act.wait_ge(wo_loaded, 16)
            act.activation(wo_hi[:], wo_stage[:], ACT.Copy).then_inc(wo_hi_ready, 1)
            for e in range(E):
                both = resident[:, e * EW:e * EW + DC * 2 * M].rearrange("p (c two m) -> p c two m", c=DC, two=2)
                down = resident[:, e * EW + DC * 2 * M:(e + 1) * EW].rearrange("p (c n) -> p c n", c=MC)
                act.dma_start(both[:, :, 0, :], w_gate[e].rearrange("(c p) m -> p c m", p=P)).then_inc(experts_loaded, 16)
                act.dma_start(both[:, :, 1, :], w_up[e].rearrange("(c p) m -> p c m", p=P)).then_inc(experts_loaded, 16)
                act.dma_start(down, w_down[e].rearrange("(c p) n -> p c n", p=P)).then_inc(experts_loaded, 16)
            split_high(0, 0)
            steps(act, step)
            copy_x1T(T - 1)
            act.wait_ge(experts_loaded, 16 * 3 * E)

        @block.tensor
        def _(pe):
            def transpose_o(t, k, m):
                pe.wait_ge(o_loaded[k], 16 * m + 16)
                if not (known(t) and t < 2):
                    pe.wait_ge(oT_lo_ready, 2 * t - 2)
                for j in range(2):
                    for c in range(4):
                        last = pe.transpose(oT_bank[k][j][:, c * P:(c + 1) * P],
                                            o_in[k][:, (4 * j + c) * P:(4 * j + c + 1) * P], ident[:])
                    last.then_inc(oT_full, 1)

            def project(t, k):
                pe.wait_ge(oT_lo_ready, 2 * t + 2)
                if not (known(t) and t < 2):
                    pe.wait_ge(y_ready, t - 1)
                for c in range(IC):
                    pe.matmul(out_bank[k], oT_hi[k][:, c, :], wo_hi[:, c, :], start=(c == 0), stop=False)
                    pe.matmul(out_bank[k], oT_hi[k][:, c, :], wo_lo[:, c, :], start=False, stop=False)
                    last = pe.matmul(out_bank[k], oT_lo[k][:, c, :], wo_hi[:, c, :], start=False, stop=(c == IC - 1))
                last.then_inc(out_full, 1)

            def transpose_x1(t, k):
                pe.wait_ge(x1_ready, t + 1)
                pe.wait_ge(x1T_copied, t)
                for c in range(DC):
                    last = pe.transpose(x1T_bank[:, c * P:(c + 1) * P], x1[k][:, c * P:(c + 1) * P], ident[:])
                last.then_inc(x1T_full, 1)

            def route(t):
                pe.wait_ge(x1T_copied, t + 1)
                for c in range(DC):
                    last = pe.matmul(logits_bank[:, bass.ds(t * E, E)], x1T[:, c, :], wt_T[:, c, :],
                                     start=(c == 0), stop=(c == DC - 1))
                last.then_inc(logits_full, 1)

            def step(t, k, m):
                if not (known(t) and t + 1 >= T):
                    transpose_o(t + 1, 1 - k, m + k)
                if not (known(t) and t < 2):
                    route(t - 2)
                project(t, k)
                if not (known(t) and t == 0):
                    transpose_x1(t - 1, 1 - k)

            transpose_o(0, 0, 0)
            pe.wait_ge(small_loaded, 16 * (3 + DC))
            for b in range(B):
                last = pe.matmul(x1T_bank[:, b * E:(b + 1) * E], cond_T[:, b:b + 1].to_broadcast([G, P]), wg_T[:],
                                 start=True, stop=True)
            last.then_inc(group_full, 1)
            pe.wait_ge(wo_lo_ready, 1)
            pe.wait_ge(group_copied, 1)
            steps(pe, step)
            route(T - 2)
            transpose_x1(T - 1, 1)
            route(T - 1)


def stage_route(nc, sw_gate, sw_up, sw_down, psum, logits, shared, route):
    with ExitStack() as ctx:
        def sb(name, shape, dt=F32):
            return ctx.enter_context(nc.sbuf_tensor(name, shape, dt))

        def sem(name):
            return ctx.enter_context(nc.semaphore(name))

        NTE = [P, T, E]
        expert_no, row_no, tile_no = sb("expert_no", [P, E]), sb("row_no", [P, P]), sb("tile_no", [P, SLOT_TILES])
        filled, token_no = sb("filled_at", [P, T]), sb("token_no", [P, TOPK * T])
        before, ones = sb("before", [P, P]), sb("ones", [P, P])
        w_stage = sb("shared_stage", [P, DC, SM])
        first, second, taken, both = sb("first", NTE), sb("second", NTE), sb("taken", NTE), sb("both", NTE)
        work, shifted, totals = sb("work", NTE), sb("shifted", NTE), sb("totals", NTE)
        runs = [sb(f"runs{i}", NTE) for i in range(2)]
        best, low = sb("best", [P, TOPK, T]), sb("low4", [P, T])
        exps, exp_sum, gap, score = sb("exps", NTE), sb("exp_sum", [P, T]), sb("gap", [P, T]), sb("score", [P, TOPK, T])
        norm = sb("norm", [P, T])
        more, tiles = sb("more", [P, E, T]), sb("tiles", [P, E])
        ends = [sb(f"ends{i}", [P, E]) for i in range(2)]
        ended, owner = sb("ended", [P, SLOT_TILES, E]), sb("owner", [P, SLOT_TILES])
        slot_f, slot_part = sb("slot_f", [P, TOPK, T]), sb("slot_part", [P, 2, TOPK * T], I32)
        slot_tile, slot_row = sb("slot_tile", [P, TOPK * T]), sb("slot_row", [P, TOPK * T])
        row_hot = [sb(f"row_hot{i}", [P, P], F32R) for i in range(4)]
        tile_hot = [sb(f"tile_hot{i}", [P, SLOT_TILES], F32R) for i in range(4)]

        iotas, step, both_ready = sem("iotas"), sem("routing_step"), sem("both_ready")
        shifted_ready, exps_ready = sem("shifted_ready"), sem("exps_ready")
        counts_full, hot_ready, hot_used = sem("counts_full"), sem("hot_ready"), sem("hot_used")
        shared_loaded, shared_hi_ready, shared_lo_ready = (sem("shared_loaded"), sem("shared_hi_ready"),
                                                           sem("shared_lo_ready"))
        PAIRS = TOPK * T
        pre_bank, total_bank, token_bank = bank(psum, 0), bank(psum, 1), bank(psum, 2)

        def grid(a):
            return a.rearrange("p (t e) -> p t e", e=E)

        block = ctx.enter_context(nc.Block())

        @block.sync
        def _(sp):
            for n, w in enumerate((sw_gate, sw_up, sw_down)):
                sp.wait_ge(shared_lo_ready, n)
                sp.dma_start(w_stage[:], w.rearrange("(c p) n -> p c n", p=P)).then_inc(shared_loaded, 16)

        @block.gpsimd
        def _(pool):
            pool.iota(expert_no[:], pattern=[[1, E]], base=0, channel_multiplier=0,
                      allow_small_or_imprecise_dtypes=True).then_inc(iotas, 1)
            pool.memset(before[:], 1.0).then_inc(iotas, 1)
            pool.memset(ones[:], 1.0).then_inc(iotas, 1)
            pool.wait_ge(iotas, 3)
            pool.affine_select(out=before[:], in_=before[:], compare_op=ALU.is_ge, fill=0.0, base=-1,
                               pattern=[[1, P]], channel_multiplier=-1).then_inc(iotas, 1)
            for out, pattern, channel in ((filled, [[P, T]], 0), (tile_no, [[1, SLOT_TILES]], 0),
                                          (row_no, [[1, P]], 0), (token_no, [[0, TOPK], [P, T]], 1)):
                pool.iota(out[:], pattern=pattern, base=0, channel_multiplier=channel,
                          allow_small_or_imprecise_dtypes=True).then_inc(iotas, 1)
            for n in range(3):
                pool.wait_ge(shared_hi_ready, n + 1)
                pool.tensor_tensor(out=shared["lo"][n][:], in0=w_stage[:], in1=shared["hi"][n][:].bitcast(F32),
                                   op=ALU.subtract).then_inc(shared_lo_ready, 1)

        @block.scalar
        def _(act):
            def split_high(n):
                act.wait_ge(shared_loaded, 16 * n + 16)
                act.activation(shared["hi"][n][:], w_stage[:], ACT.Copy).then_inc(shared_hi_ready, 1)

            split_high(0)
            act.wait_ge(shifted_ready, 2)
            act.activation(exps[:], shifted[:], ACT.Exp, scale=0.5).then_inc(exps_ready, 1)
            act.activation(score[:, 1, :], gap[:], ACT.Exp, scale=0.5).then_inc(exps_ready, 1)
            split_high(1)
            split_high(2)

        @block.vector
        def _(dve):
            done = [0]

            def then(instruction):
                done[0] += 1
                instruction.then_inc(step, 1)
                dve.wait_ge(step, done[0])

            def over_experts(a):
                return a.unsqueeze(2).to_broadcast(NTE)

            def over_tiles(a):
                return a.unsqueeze(1).to_broadcast(NTE)

            def pick(hot, values, n):
                then(dve.tensor_reduce(out=best[:, n, :], in_=values[:], axis=AX.X, op=ALU.max))
                then(dve.tensor_tensor(out=work[:], in0=values[:], in1=over_experts(best[:, n, :]), op=ALU.is_equal))
                then(dve.scalar_tensor_tensor(out=work[:], in0=work[:], scalar=-float(E), in1=over_tiles(expert_no[:]),
                                              op0=ALU.mult, op1=ALU.add))
                then(dve.tensor_reduce(out=low[:], in_=work[:], axis=AX.X, op=ALU.min))
                then(dve.tensor_tensor(out=hot[:], in0=work[:], in1=over_experts(low[:]), op=ALU.is_equal))

            dve.wait_ge(iotas, 8)
            pick(first, logits, 0)
            then(dve.scalar_tensor_tensor(out=taken[:], in0=first[:], scalar=-MASKED, in1=logits[:], op0=ALU.mult,
                                          op1=ALU.add))
            pick(second, taken, 1)
            dve.tensor_tensor(out=both[:], in0=first[:], in1=second[:], op=ALU.add).then_inc(both_ready, 1)
            dve.tensor_tensor(out=shifted[:], in0=logits[:], in1=over_experts(best[:, 0, :]), op=ALU.subtract
                              ).then_inc(shifted_ready, 1)
            dve.tensor_tensor(out=gap[:], in0=best[:, 1, :], in1=best[:, 0, :], op=ALU.subtract
                              ).then_inc(shifted_ready, 1)
            dve.wait_ge(counts_full, 1)
            dve.tensor_copy(totals[:], grid(total_bank[:, 0:T * E]))
            then(dve.tensor_copy(runs[0][:], grid(total_bank[:, 0:T * E])))
            src, far = 0, 1
            while far < T:
                dve.tensor_copy(runs[1 - src][:, 0:far, :], runs[src][:, 0:far, :]).then_inc(step, 1)
                done[0] += 1
                then(dve.tensor_tensor(out=runs[1 - src][:, far:T, :], in0=runs[src][:, far:T, :],
                                       in1=runs[src][:, 0:T - far, :], op=ALU.add))
                src, far = 1 - src, 2 * far
            then(dve.tensor_tensor(out=more[:], in0=runs[src][:, T - 1, :].unsqueeze(2).to_broadcast([P, E, T]),
                                   in1=filled[:].unsqueeze(1).to_broadcast([P, E, T]), op=ALU.is_gt))
            then(dve.tensor_reduce(out=tiles[:], in_=more[:], axis=AX.X, op=ALU.add))
            then(dve.tensor_copy(ends[0][:], tiles[:]))
            end, far = 0, 1
            while far < E:
                dve.tensor_copy(ends[1 - end][:, 0:far], ends[end][:, 0:far]).then_inc(step, 1)
                done[0] += 1
                then(dve.tensor_tensor(out=ends[1 - end][:, far:E], in0=ends[end][:, far:E], in1=ends[end][:, 0:E - far],
                                       op=ALU.add))
                end, far = 1 - end, 2 * far
            then(dve.tensor_tensor(out=ended[:], in0=ends[end][:].unsqueeze(1).to_broadcast([P, SLOT_TILES, E]),
                                   in1=tile_no[:].unsqueeze(2).to_broadcast([P, SLOT_TILES, E]), op=ALU.is_le))
            then(dve.tensor_reduce(out=owner[:], in_=ended[:], axis=AX.X, op=ALU.add))
            then(dve.tensor_scalar(out=route["experts"][:], in0=owner[0:1, :], scalar1=float(E - 1), scalar2=None,
                                   op0=ALU.min))
            then(dve.tensor_tensor(out=tiles[:], in0=ends[end][:], in1=tiles[:], op=ALU.subtract))
            then(dve.tensor_scalar(out=tiles[:], in0=tiles[:], scalar1=float(P), scalar2=None, op0=ALU.mult))
            then(dve.tensor_tensor(out=work[:], in0=runs[src][:], in1=totals[:], op=ALU.subtract))
            then(dve.tensor_tensor(out=work[:], in0=work[:], in1=over_tiles(tiles[:]), op=ALU.add))
            then(dve.tensor_tensor(out=work[:], in0=grid(pre_bank[:, 0:T * E]), in1=work[:], op=ALU.add))
            for n, hot in enumerate((first, second)):
                then(dve.tensor_tensor(out=taken[:], in0=hot[:], in1=work[:], op=ALU.mult))
                then(dve.tensor_reduce(out=slot_f[:, n, :], in_=taken[:], axis=AX.X, op=ALU.add))
            then(dve.tensor_copy(route["slots"][:], slot_f[:]))
            flat = route["slots"][:].rearrange("p k t -> p (k t)")
            dve.tensor_scalar(out=slot_part[:, 0, :], in0=flat, scalar1=7, scalar2=None, op0=ALU.arith_shift_right
                              ).then_inc(step, 1)
            done[0] += 1
            then(dve.tensor_scalar(out=slot_part[:, 1, :], in0=flat, scalar1=P - 1, scalar2=None, op0=ALU.bitwise_and))
            dve.tensor_copy(slot_tile[:], slot_part[:, 0, :]).then_inc(step, 1)
            done[0] += 1
            then(dve.tensor_copy(slot_row[:], slot_part[:, 1, :]))
            with dve.Fori(0, PAIRS // 4) as g:
                dve.wait_ge(hot_used, 4 * g)
                for k in range(4):
                    dve.tensor_scalar(out=row_hot[k][:], in0=row_no[:], scalar1=slot_row[:, bass.ds(4 * g + k, 1)],
                                      scalar2=None, op0=ALU.is_equal).then_inc(hot_ready, 1)
                    dve.tensor_scalar(out=tile_hot[k][:], in0=tile_no[:], scalar1=slot_tile[:, bass.ds(4 * g + k, 1)],
                                      scalar2=token_no[:, bass.ds(4 * g + k, 1)], op0=ALU.is_equal, op1=ALU.mult
                                      ).then_inc(hot_ready, 1)
            dve.wait_ge(exps_ready, 2)
            then(dve.tensor_reduce(out=exp_sum[:], in_=exps[:], axis=AX.X, op=ALU.add))
            then(dve.reciprocal(score[:, 0, :], exp_sum[:]))
            then(dve.tensor_tensor(out=score[:, 1, :], in0=score[:, 1, :], in1=score[:, 0, :], op=ALU.mult))
            then(dve.tensor_tensor(out=norm[:], in0=score[:, 0, :], in1=score[:, 1, :], op=ALU.add))
            then(dve.tensor_scalar(out=norm[:], in0=norm[:], scalar1=TINY, scalar2=None, op0=ALU.add))
            then(dve.reciprocal(exp_sum[:], norm[:]))
            then(dve.tensor_tensor(out=route["weights"][:], in0=score[:],
                                   in1=exp_sum[:].unsqueeze(1).to_broadcast([P, TOPK, T]), op=ALU.mult))
            dve.wait_ge(hot_used, PAIRS)
            then(dve.tensor_copy(route["tokens"][:], token_bank[:, 0:SLOT_TILES]))

        @block.tensor
        def _(pe):
            pe.wait_ge(both_ready, 1)
            pe.wait_ge(iotas, 4)
            flat = both[:].rearrange("p t e -> p (t e)")
            pe.matmul(pre_bank[:, 0:T * E], before[:], flat, start=True, stop=True)
            pe.matmul(total_bank[:, 0:T * E], ones[:], flat, start=True, stop=True).then_inc(counts_full, 1)

            def add_pair(k, at, start, stop):
                pe.wait_ge(hot_ready, at)
                pe.matmul(token_bank[:, 0:SLOT_TILES], row_hot[k][:], tile_hot[k][:], start=start, stop=stop
                          ).then_inc(hot_used, 1)

            for k in range(4):
                add_pair(k, 2 * k + 2, k == 0, False)
            with pe.Fori(1, PAIRS // 4 - 1) as g:
                for k in range(4):
                    add_pair(k, 8 * g + 2 * k + 2, False, False)
            for k in range(4):
                add_pair(k, 2 * PAIRS - 8 + 2 * k + 2, False, k == 3)


def stage_experts(nc, dram, psum, resident, ident, spare, route):
    with ExitStack() as ctx:
        def sb(name, shape, dt=F32):
            return ctx.enter_context(nc.sbuf_tensor(name, shape, dt))

        def sem(name):
            return ctx.enter_context(nc.semaphore(name))

        rows = [sb(f"slot_rows{i}", [P, 1], I32) for i in range(2)]
        xg = [sb(f"xg{i}", [P, D]) for i in range(2)]
        xT = [sb(f"xT5_{i}", [P, DC, P]) for i in range(2)]
        leak = [sb(f"leak{i}", [P, M]) for i in range(2)]
        hidden = [sb(f"hidden{i}", [P, M]) for i in range(2)]
        hT = [sb(f"hT{i}", [P, MC, P]) for i in range(2)]
        y_out = [sb(f"y_out{i}", [P, D]) for i in range(2)]

        rows_ready = sem("rows_ready")
        xg_loaded = [sem(f"xg_loaded{i}") for i in range(2)]
        xT_full, xT_copied, up_full = sem("xT5_full"), sem("xT5_copied"), sem("gate_up_full")
        leak_ready, leaky_ready, hidden_ready = sem("leak_ready"), sem("leaky_ready"), sem("hidden_ready")
        hT_full, hT_copied, y_full, y_copied = sem("hT_full"), sem("hT_copied"), sem("y_full"), sem("y_copied")
        ys_stored = [sem(f"ys_stored{i}") for i in range(2)]

        xT_bank, up_bank = [bank(psum, k) for k in (0, 1)], [bank(psum, k) for k in (2, 3)]
        hT_bank, y_bank = [bank(psum, k) for k in (4, 5)], [bank(psum, k) for k in (6, 7)]
        N = SLOT_TILES

        def steps(eng, step):
            step(0, 0, 0)
            step(1, 1, 0)
            with eng.Fori(1, N // 2 - 1) as m:
                for k in range(2):
                    step(2 * m + k, k, m)
            step(N - 2, 0, N // 2 - 1)
            step(N - 1, 1, N // 2 - 1)

        def known(s):
            return isinstance(s, int)

        def has_next(s):
            return not (known(s) and s + 1 >= N)

        def has_last(s):
            return not (known(s) and s == 0)

        def from_third(s):
            return not (known(s) and s < 2)

        block = ctx.enter_context(nc.Block())

        @block.gpsimd
        def _(pool):
            def step(s, k, m):
                if from_third(s):
                    pool.wait_ge(xT_full, s - 1)
                pool.tensor_copy(rows[k][:], route["tokens"][:, bass.ds(s, 1)]).then_inc(rows_ready, 1)
                pool.wait_ge(rows_ready, s + 1)
                pool.tensor_tensor(out=spare["pool"][:, 0:1], in0=ident[0:1, 0:1], in1=ident[0:1, 0:1], op=ALU.mult)
                pool.indirect_dma_start(out=xg[k][:], out_offset=None, in_=dram["x1"],
                                        in_offset=bass.IndirectOffsetOnAxis(ap=rows[k][:].bitcast(U32), axis=0)
                                        ).then_inc(xg_loaded[k], 16)

            steps(pool, step)

        @block.sync
        def _(sp):
            def step(s, k, m):
                sp.wait_ge(y_copied, s + 1)
                sp.dma_start(dram["ys"][bass.ds(s * P, P), :], y_out[k][:]).then_inc(ys_stored[k], 16)

            steps(sp, step)
            for k in range(2):
                sp.wait_ge(ys_stored[k], 16 * N // 2)

        @block.scalar
        def _(act):
            def copy_xT(s, k):
                act.wait_ge(xT_full, s + 1)
                if from_third(s):
                    act.wait_ge(up_full, s - 1)
                act.activation(xT[k][:].rearrange("p c n -> p (c n)"), xT_bank[k], ACT.Copy).then_inc(xT_copied, 1)

            def copy_y(s, k, m):
                act.wait_ge(y_full, s + 1)
                act.wait_ge(ys_stored[k], 16 * m)
                act.activation(y_out[k][:], y_bank[k], ACT.Copy).then_inc(y_copied, 1)

            def step(s, k, m):
                act.wait_ge(up_full, s + 1)
                if from_third(s):
                    act.wait_ge(hidden_ready, s - 1)
                act.activation(leak[k][:], up_bank[k][:, 0:M], ACT.Copy, scale=LEAK).then_inc(leak_ready, 1)
                if has_next(s):
                    copy_xT(s + 1, 1 - k)
                if has_last(s):
                    copy_y(s - 1, 1 - k, m + k - 1)

            copy_xT(0, 0)
            steps(act, step)
            copy_y(N - 1, 1, N // 2 - 1)

        @block.vector
        def _(dve):
            def copy_hT(s, k):
                dve.wait_ge(hT_full, s + 1)
                if from_third(s):
                    dve.wait_ge(y_full, s - 1)
                dve.tensor_copy(hT[k][:].rearrange("p c n -> p (c n)"), hT_bank[k][:, 0:M]).then_inc(hT_copied, 1)

            def step(s, k, m):
                if has_last(s):
                    copy_hT(s - 1, 1 - k)
                dve.wait_ge(leak_ready, s + 1)
                dve.tensor_tensor(out=leak[k][:], in0=up_bank[k][:, 0:M], in1=leak[k][:], op=ALU.max
                                  ).then_inc(leaky_ready, 1)
                dve.wait_ge(leaky_ready, s + 1)
                if from_third(s):
                    dve.wait_ge(hT_full, s - 1)
                dve.tensor_tensor(out=hidden[k][:], in0=up_bank[k][:, M:2 * M], in1=leak[k][:], op=ALU.mult
                                  ).then_inc(hidden_ready, 1)

            steps(dve, step)
            copy_hT(N - 1, 1)

        @block.tensor
        def _(pe):
            def weights_at(s):
                e = pe.value_load(route["experts"][0:1, bass.ds(s, 1)], min_val=0, max_val=E - 1)
                return e * EW

            def transpose_x(s, k, m):
                pe.wait_ge(xg_loaded[k], 16 * m + 16)
                if from_third(s):
                    pe.wait_ge(xT_copied, s - 1)
                for c in range(DC):
                    last = pe.transpose(xT_bank[k][:, c * P:(c + 1) * P], xg[k][:, c * P:(c + 1) * P], ident[:])
                last.then_inc(xT_full, 1)

            def gate_up(s, k):
                at = weights_at(s)
                pe.wait_ge(xT_copied, s + 1)
                if from_third(s):
                    pe.wait_ge(hidden_ready, s - 1)
                for c in range(DC):
                    last = pe.matmul(up_bank[k], xT[k][:, c, :], resident[:, bass.ds(at + c * 2 * M, 2 * M)],
                                     start=(c == 0), stop=(c == DC - 1))
                last.then_inc(up_full, 1)

            def transpose_h(s, k):
                pe.wait_ge(hidden_ready, s + 1)
                if from_third(s):
                    pe.wait_ge(hT_copied, s - 1)
                for c in range(MC):
                    last = pe.transpose(hT_bank[k][:, c * P:(c + 1) * P], hidden[k][:, c * P:(c + 1) * P], ident[:])
                last.then_inc(hT_full, 1)

            def down(s, k):
                at = weights_at(s)
                pe.wait_ge(hT_copied, s + 1)
                if from_third(s):
                    pe.wait_ge(y_copied, s - 1)
                for c in range(MC):
                    last = pe.matmul(y_bank[k], hT[k][:, c, :], resident[:, bass.ds(at + DC * 2 * M + c * D, D)],
                                     start=(c == 0), stop=(c == MC - 1))
                last.then_inc(y_full, 1)

            def step(s, k, m):
                gate_up(s, k)
                if has_last(s):
                    transpose_h(s - 1, 1 - k)
                if has_next(s):
                    transpose_x(s + 1, 1 - k, m + k)
                if has_last(s):
                    down(s - 1, 1 - k)

            transpose_x(0, 0, 0)
            steps(pe, step)
            transpose_h(N - 1, 1)
            down(N - 1, 1)


def stage_shared(nc, dram, psum, resident, ident, spare, shared, route, out):
    with ExitStack() as ctx:
        def sb(name, shape, dt=F32):
            return ctx.enter_context(nc.sbuf_tensor(name, shape, dt))

        def sem(name):
            return ctx.enter_context(nc.semaphore(name))

        at = [0]

        def reuse(*shape):
            n = 1
            for d in shape:
                n *= d
            at[0] += n
            flat = resident[:, at[0] - n:at[0]]
            return flat if len(shape) == 1 else flat.rearrange("p (a b) -> p a b", a=shape[0])

        x1 = [reuse(TB, D) for _ in range(2)]
        leak = [reuse(S) for _ in range(2)]
        hidden = [reuse(S) for _ in range(2)]
        picked = [[reuse(D) for _ in range(TOPK)] for _ in range(2)]
        total = [reuse(D) for _ in range(2)]
        xT_hi = [sb(f"xT6_hi{i}", [P, DC, S], F32R) for i in range(2)]
        xT_lo = [sb(f"xT6_lo{i}", [P, DC, S], F32R) for i in range(2)]
        h_hi, h_lo = sb("h_hi", [P, SC, S], F32R), sb("h_lo", [P, SC, S], F32R)
        rows = [sb(f"picked_rows{i}", [P, TOPK], I32) for i in range(2)]

        x1_loaded = [sem(f"x1_loaded{i}") for i in range(2)]
        xT_full, xT_hi_ready, xT_lo_ready = sem("xT6_full"), sem("xT6_hi_ready"), sem("xT6_lo_ready")
        up_full, leak_ready, leaky_ready, hidden_ready = (sem("up6_full"), sem("leak6_ready"), sem("leaky6_ready"),
                                                          sem("hidden6_ready"))
        h_hi_ready, h_lo_ready, y_full = sem("h_hi_ready"), sem("h_lo_ready"), sem("y6_full")
        rows_ready = sem("picked_rows_ready")
        picked_loaded = [sem(f"picked_loaded{i}") for i in range(2)]
        y_added, first_added, total_ready = sem("y_added"), sem("first_added"), sem("total_ready")
        out_stored = [sem(f"out_stored{i}") for i in range(2)]

        out_rows = out.rearrange("b s d -> (b s) d")
        xT_bank, gate_bank = [bank(psum, k) for k in (0, 1)], [bank(psum, k) for k in (2, 3)]
        up_bank, y_bank = [bank(psum, k) for k in (4, 5)], [bank(psum, k) for k in (6, 7)]
        (gate_hi, up_hi, down_hi), (gate_lo, up_lo, down_lo) = shared["hi"], shared["lo"]

        def batches(eng, step):
            step(0, 0, 0)
            step(1, 1, 0)
            with eng.Fori(1, B // 2 - 1) as m:
                for k in range(2):
                    step(2 * m + k, k, m)
            step(B - 2, 0, B // 2 - 1)
            step(B - 1, 1, B // 2 - 1)

        def known(b):
            return isinstance(b, int)

        block = ctx.enter_context(nc.Block())

        @block.sync
        def _(sp):
            def load_x1(b, k):
                sp.dma_start(x1[k], dram["x1"][bass.ds(b * S, S), :].rearrange("(t p) d -> p t d", p=P)
                             ).then_inc(x1_loaded[k], 16)

            def step(b, k, m):
                for t in range(TB):
                    sp.wait_ge(total_ready, TB * b + t + 1)
                    sp.dma_start(out_rows[bass.ds(b * S + t * P, P), :], total[t % 2]).then_inc(out_stored[t % 2], 16)
                if not (known(b) and b + 2 >= B):
                    load_x1(b + 2, k)

            load_x1(0, 0)
            load_x1(1, 1)
            batches(sp, step)
            for k in range(2):
                sp.wait_ge(out_stored[k], 16 * T // 2)

        @block.gpsimd
        def _(pool):
            def step(b, k, m):
                for t in range(TB):
                    n = t % 2
                    if not (known(b) and b == 0 and t < 2):
                        pool.wait_ge(total_ready, TB * b + t - 1)
                    pool.tensor_copy(rows[n][:], route["slots"][:, :, bass.ds(TB * b + t, 1)].rearrange("p k a -> p (k a)")
                                     ).then_inc(rows_ready, 1)
                    pool.wait_ge(rows_ready, TB * b + t + 1)
                    pool.tensor_tensor(out=spare["pool"][:, 0:1], in0=ident[0:1, 0:1], in1=ident[0:1, 0:1], op=ALU.mult)
                    for j in range(TOPK):
                        pool.indirect_dma_start(out=picked[n][j], out_offset=None, in_=dram["ys"],
                                                in_offset=bass.IndirectOffsetOnAxis(ap=rows[n][:, j:j + 1].bitcast(U32),
                                                                                    axis=0)
                                                ).then_inc(picked_loaded[n], 16)

            batches(pool, step)

        @block.scalar
        def _(act):
            def split_x_high(b, k):
                if not (known(b) and b < 2):
                    act.wait_ge(up_full, SC * b - SC)
                for c in range(DC):
                    act.wait_ge(xT_full, DC * b + c + 1)
                    act.activation(xT_hi[k][:, c, :], xT_bank[c % 2], ACT.Copy).then_inc(xT_hi_ready, 1)

            def step(b, k, m):
                for j in range(SC):
                    act.wait_ge(up_full, SC * b + j + 1)
                    if not (known(b) and b == 0 and j < 2):
                        act.wait_ge(h_lo_ready, SC * b + j - 1)
                    act.activation(leak[j % 2], gate_bank[j % 2], ACT.Copy, scale=LEAK).then_inc(leak_ready, 1)
                    act.wait_ge(hidden_ready, SC * b + j + 1)
                    if j == 0:
                        act.wait_ge(y_full, TB * b)
                    act.activation(h_hi[:, j, :], hidden[j % 2], ACT.Copy).then_inc(h_hi_ready, 1)
                if not (known(b) and b + 1 >= B):
                    split_x_high(b + 1, 1 - k)

            split_x_high(0, 0)
            batches(act, step)

        @block.vector
        def _(dve):
            def split_x_low(b, k):
                for c in range(DC):
                    dve.wait_ge(xT_hi_ready, DC * b + c + 1)
                    dve.tensor_tensor(out=xT_lo[k][:, c, :], in0=xT_bank[c % 2], in1=xT_hi[k][:, c, :].bitcast(F32),
                                      op=ALU.subtract).then_inc(xT_lo_ready, 1)

            def step(b, k, m):
                for j in range(SC):
                    dve.wait_ge(leak_ready, SC * b + j + 1)
                    dve.tensor_tensor(out=leak[j % 2], in0=gate_bank[j % 2], in1=leak[j % 2], op=ALU.max
                                      ).then_inc(leaky_ready, 1)
                    dve.wait_ge(leaky_ready, SC * b + j + 1)
                    dve.tensor_tensor(out=hidden[j % 2], in0=up_bank[j % 2], in1=leak[j % 2], op=ALU.mult
                                      ).then_inc(hidden_ready, 1)
                    dve.wait_ge(h_hi_ready, SC * b + j + 1)
                    dve.tensor_tensor(out=h_lo[:, j, :], in0=hidden[j % 2], in1=h_hi[:, j, :].bitcast(F32),
                                      op=ALU.subtract).then_inc(h_lo_ready, 1)
                if not (known(b) and b + 1 >= B):
                    split_x_low(b + 1, 1 - k)
                for t in range(TB):
                    n = t % 2
                    done = TB * b + t + 1
                    dve.wait_ge(y_full, done)
                    dve.wait_ge(out_stored[n], 16 * (TB // 2 * b + t // 2))
                    dve.tensor_tensor(out=total[n], in0=y_bank[n], in1=x1[k][:, t, :], op=ALU.add).then_inc(y_added, 1)
                    dve.wait_ge(y_added, done)
                    dve.wait_ge(picked_loaded[n], 16 * TOPK * (TB // 2 * b + t // 2 + 1))
                    for j, added in enumerate((first_added, total_ready)):
                        dve.scalar_tensor_tensor(out=total[n], in0=picked[n][j],
                                                 scalar=route["weights"][:, j, bass.ds(TB * b + t, 1)], in1=total[n],
                                                 op0=ALU.mult, op1=ALU.add).then_inc(added, 1)
                        if j == 0:
                            dve.wait_ge(first_added, done)

            split_x_low(0, 0)
            batches(dve, step)

        @block.tensor
        def _(pe):
            def transpose_x(b, k, m):
                pe.wait_ge(x1_loaded[k], 16 * m + 16)
                for c in range(DC):
                    if not (known(b) and b == 0 and c < 2):
                        pe.wait_ge(xT_lo_ready, DC * b + c - 1)
                    for t in range(TB):
                        last = pe.transpose(xT_bank[c % 2][:, t * P:(t + 1) * P], x1[k][:, t, c * P:(c + 1) * P], ident[:])
                    last.then_inc(xT_full, 1)

            def three(out, hi, lo, rhs_hi, rhs_lo, start, stop):
                pe.matmul(out, hi, rhs_hi, start=start, stop=False)
                pe.matmul(out, hi, rhs_lo, start=False, stop=False)
                return pe.matmul(out, lo, rhs_hi, start=False, stop=stop)

            def step(b, k, m):
                pe.wait_ge(xT_lo_ready, DC * b + DC)
                for j in range(SC):
                    if not (known(b) and b == 0 and j < 2):
                        pe.wait_ge(hidden_ready, SC * b + j - 1)
                    cols = slice(j * P, (j + 1) * P)
                    for dst, hi, lo in ((gate_bank, gate_hi, gate_lo), (up_bank, up_hi, up_lo)):
                        for c in range(DC):
                            last = three(dst[j % 2], hi[:, c, cols], lo[:, c, cols], xT_hi[k][:, c, :], xT_lo[k][:, c, :],
                                         c == 0, c == DC - 1)
                    last.then_inc(up_full, 1)
                if not (known(b) and b + 1 >= B):
                    transpose_x(b + 1, 1 - k, m + k)
                pe.wait_ge(h_lo_ready, SC * b + SC)
                for t in range(TB):
                    if not (known(b) and b == 0 and t < 2):
                        pe.wait_ge(y_added, TB * b + t - 1)
                    rows = slice(t * P, (t + 1) * P)
                    for j in range(SC):
                        last = three(y_bank[t % 2], h_hi[:, j, rows], h_lo[:, j, rows], down_hi[:, j, :], down_lo[:, j, :],
                                     j == 0, j == SC - 1)
                    last.then_inc(y_full, 1)

            transpose_x(0, 0, 0)
            batches(pe, step)


_INS = ['x', 'fside_16xSxS_0', 'cond_64', 'mask_BxS_bk0', 'L0_cond_g_in', 'L0_cond_null_attn_bias', 'L0_cond_Wq',
        'L0_cond_Wkv', 'L0_cond_Wo', 'L0_cond_g_out', 'L1_cond_wt', 'L1_cond_wg', 'L1_cond_w_gate', 'L1_cond_w_up',
        'L1_cond_w_down', 'L1_cond_sw_gate', 'L1_cond_sw_up', 'L1_cond_sw_down']


def kernel(**inputs):
    import numpy as np
    import concourse.bacc as bacc
    from concourse.bass_utils import run_bass_kernel_spmd

    nc = bacc.Bacc("TRN2", target_bir_lowering=False, num_devices=1)
    arrays, args = {}, []
    for name in _INS:
        a = np.ascontiguousarray(inputs[name])
        arrays[f"in_{name}"] = a
        args.append(nc.dram_tensor(f"in_{name}", a.shape, mybir.dt.from_np(a.dtype), kind="ExternalInput").ap())
    out = nc.dram_tensor("out", (B, S, D), F32, kind="ExternalOutput").ap()
    build(nc, *args, out)
    r = run_bass_kernel_spmd(nc, [arrays], core_ids=[0])
    return r.results[0]["out"]
```

```python
import concourse.bass as bass
from concourse import mybir
from contextlib import ExitStack

F32 = mybir.dt.float32
F32R = mybir.dt.float32r
I32 = mybir.dt.int32
U8 = mybir.dt.uint8
U32 = mybir.dt.uint32
ALU = mybir.AluOpType
ACT = mybir.ActivationFunctionType
AX = mybir.AxisListType

P = 128
B, S, D = 8, 512, 512
H, DH = 16, 64
INNER = H * DH
TB = S // P
T = B * TB
DC = D // P
IC = INNER // P
E, M, TOPK = 8, 256, 2
SM = 2 * M
SC = SM // P
MC = M // P
G = 64
SLOT_TILES = T * TOPK + E
EPS = 1e-5
TINY = 1e-20
LEAK = 0.01
MASKED = 2.0 ** 120
BANK = 512
HALF = H // 2
AHEAD = 2
CK = [AHEAD + P * (i + 1) for i in range(TB)]
BIAS_AT = [H * sum(CK[:i]) for i in range(TB)]
PLACES = 3
EW = DC * 2 * M + MC * D


def build(nc, x, fside, cond, mask, g_in, null_bias, Wq, Wkv, Wo, g_out,
          wt, wg, w_gate, w_up, w_down, sw_gate, sw_up, sw_down, out):
    dram = {
        "q_hi": nc.dram_tensor("q_hi_d", (B, INNER, S), F32, kind="Internal").ap(),
        "q_lo": nc.dram_tensor("q_lo_d", (B, INNER, S), F32, kind="Internal").ap(),
        "k_hi": nc.dram_tensor("k_hi_d", (B, DH, S), F32, kind="Internal").ap(),
        "k_lo": nc.dram_tensor("k_lo_d", (B, DH, S), F32, kind="Internal").ap(),
        "mask": nc.dram_tensor("mask_d", (1, B * S), F32, kind="Internal").ap(),
        "o": nc.dram_tensor("o_d", (B * S, INNER), F32, kind="Internal").ap(),
        "x1": nc.dram_tensor("x1_d", (B * S, D), F32, kind="Internal").ap(),
        "w_hi": nc.dram_tensor("w_hi_d", (E, P, EW), F32, kind="Internal").ap(),
        "w_lo": nc.dram_tensor("w_lo_d", (E, P, EW), F32, kind="Internal").ap(),
        "ys": nc.dram_tensor("ys_d", (SLOT_TILES * P, D), F32, kind="Internal").ap(),
    }
    with ExitStack() as ctx:
        psum = ctx.enter_context(nc.psum_tensor("psum", [P, 8 * BANK], F32))
        ident = ctx.enter_context(nc.sbuf_tensor("ident", [P, P], F32))
        pow_half = ctx.enter_context(nc.sbuf_tensor("pow_half", [P, TB], F32))
        eps = ctx.enter_context(nc.sbuf_tensor("eps", [P, TB], F32))
        spare = {eng: ctx.enter_context(nc.sbuf_tensor(f"spare_{eng}", [1, TB], F32)) for eng in ("dve", "pool")}
        constants_set = ctx.enter_context(nc.semaphore("constants_set"))
        stage_constants(nc, ident, pow_half, eps, constants_set)
        logits = ctx.enter_context(nc.sbuf_tensor("logits", [P, T, E], F32))
        route = {
            "weights": ctx.enter_context(nc.sbuf_tensor("top_weights", [P, TOPK, T], F32)),
            "slots": ctx.enter_context(nc.sbuf_tensor("slots", [P, TOPK, T], I32)),
            "tokens": ctx.enter_context(nc.sbuf_tensor("slot_tokens", [P, SLOT_TILES], I32)),
            "experts": ctx.enter_context(nc.sbuf_tensor("tile_experts", [1, SLOT_TILES], I32)),
            "ends": ctx.enter_context(nc.sbuf_tensor("expert_ends", [1, E], I32)),
        }
        with ExitStack() as held:
            wo_last = held.enter_context(nc.sbuf_tensor("wo_last", [P, D], F32))
            resident = held.enter_context(nc.sbuf_tensor("resident", [P, BIAS_AT[-1] + H * CK[-1] + (IC - 1) * D], F32))
            at = BIAS_AT[-1] + H * CK[-1]
            wo_stage = [resident[:, at:at + (IC - 1) * D].rearrange("p (c n) -> p c n", c=IC - 1), wo_last[:].unsqueeze(1)]
            wo_loaded = held.enter_context(nc.semaphore("wo_loaded"))
            with ExitStack() as attention:
                values = attention.enter_context(nc.sbuf_tensor("values", [P, B, TB, DH], F32))
                stage_project(nc, x, fside, cond, mask, g_in, null_bias, Wq, Wkv, dram, psum, resident, ident,
                              pow_half, eps, spare, values)
                stage_attend(nc, cond, w_gate, w_up, w_down, dram, psum, resident, ident, spare, values, Wo, wo_stage,
                             wo_loaded)
            stage_output(nc, x, cond, wo_stage, wo_loaded, g_out, wt, wg, dram, psum, ident, pow_half, eps, spare, logits)
        shared = {half: [ctx.enter_context(nc.sbuf_tensor(f"shared_{half}{n}", [P, DC, SM], F32R)) for n in range(3)]
                  for half in ("hi", "lo")}
        x1 = [ctx.enter_context(nc.sbuf_tensor(f"x1_in{i}", [P, TB, D], F32)) for i in range(2)]
        x1_loaded = [ctx.enter_context(nc.semaphore(f"x1_loaded{i}")) for i in range(2)]
        with ExitStack() as held:
            experts = held.enter_context(nc.sbuf_tensor("expert_weights", [P, PLACES * 2 * EW], F32R))
            experts_loaded = [held.enter_context(nc.semaphore(f"experts_loaded{i}")) for i in range(PLACES)]
            stage_route(nc, sw_gate, sw_up, sw_down, dram, psum, logits, shared, route, experts, experts_loaded)
            stage_experts(nc, dram, psum, ident, spare, experts, experts_loaded, route, x1, x1_loaded)
        stage_shared(nc, dram, psum, ident, spare, shared, route, x1, x1_loaded, out)


def load_x1(eng, dram, x1, b, k, x1_loaded):
    eng.dma_start(x1[k][:], dram["x1"][bass.ds(b * S, S), :].rearrange("(t p) d -> p t d", p=P)
                  ).then_inc(x1_loaded[k], 16)


def load_expert(eng, dram, experts, e, experts_loaded):
    at = e % PLACES * 2 * EW
    for n, half in enumerate(("w_hi", "w_lo")):
        eng.dma_start(experts[:, at + n * EW:at + (n + 1) * EW].bitcast(F32), dram[half][e]
                      ).then_inc(experts_loaded[e % PLACES], 16)


def bank(psum, i):
    return psum[:, i * BANK:(i + 1) * BANK]


def bias_of(resident, i, h):
    at = BIAS_AT[i] + h * CK[i]
    return resident[:, at:at + CK[i]]


def stage_constants(nc, ident, pow_half, eps, constants_set):
    with nc.Block() as block:
        @block.gpsimd
        def _(pool):
            pool.memset(ident[:], 0.0).then_inc(constants_set, 1)
            pool.memset(pow_half[:], -0.5).then_inc(constants_set, 1)
            pool.memset(eps[:], EPS).then_inc(constants_set, 1)
            pool.wait_ge(constants_set, 3)
            pool.affine_select(out=ident[:], in_=ident[:], compare_op=ALU.not_equal, fill=1.0, base=0,
                               pattern=[[-1, P]], channel_multiplier=1).then_inc(constants_set, 1)


def stage_project(nc, x, fside, cond, mask, g_in, null_bias, Wq, Wkv, dram, psum, resident, ident, pow_half,
                  eps, spare, values):
    with ExitStack() as ctx:
        def sb(name, shape, dt=F32):
            return ctx.enter_context(nc.sbuf_tensor(name, shape, dt))

        def sem(name):
            return ctx.enter_context(nc.semaphore(name))

        wq_hi, wq_lo = sb("wq_hi", [P, DC, INNER], F32R), sb("wq_lo", [P, DC, INNER], F32R)
        wkv_hi, wkv_lo = sb("wkv_hi", [P, DC, 2 * DH], F32R), sb("wkv_lo", [P, DC, 2 * DH], F32R)
        g_col = sb("g_col", [P, DC])
        xin = sb("xin", [P, TB, D])
        stats, moments, rstd = sb("stats", [P, TB, 6]), sb("moments", [P, TB, 2]), sb("rstd", [P, TB])
        xT_hi = [sb(f"xT_hi{i}", [P, DC, S], F32R) for i in range(2)]
        xT_lo = [sb(f"xT_lo{i}", [P, DC, S], F32R) for i in range(2)]
        q_hi, q_lo = sb("q_hi", [P, 2, S], F32R), sb("q_lo", [P, 2, S], F32R)
        k_hi, k_lo = sb("k_hi", [DH, S], F32R), sb("k_lo", [DH, S], F32R)
        kv_out = sb("kv_out", [P, S])
        wq_rest = sb("wq_rest", [P, DC, INNER // 2])
        null_bias_sb = sb("null_bias_sb", [P, H])
        at = BIAS_AT[-1] + H * CK[-1]
        wq_stage = [resident[:, at:at + INNER * DC // 2].rearrange("p (c n) -> p c n", c=DC),
                    wq_rest[:]]
        at += INNER * DC // 2
        wkv_stage = resident[:, at:at + DC * 2 * DH].rearrange("p (c n) -> p c n", c=DC)
        at += DC * 2 * DH
        mask_in = resident[0:T, at:at + P // 4].bitcast(U8)
        mask_out = sb("mask_out", [T, P])

        loaded = sem("small_inputs_loaded")
        wq_loaded, wkv_loaded = [sem(f"wq_loaded{j}") for j in range(2)], sem("wkv_loaded")
        bias_loaded = [sem(f"bias_loaded{i}") for i in range(TB)]
        bias_ready = sem("bias_ready")
        weights_hi, weights_lo = sem("weights_hi"), sem("weights_lo")
        x_loaded = sem("x_loaded")
        ln_stats, ln_moments, ln_shifted, ln_rstd = sem("ln_stats"), sem("ln_moments"), sem("ln_shifted"), sem("ln_rstd")
        xn_ready = sem("xn_ready")
        xT_full, xT_hi_ready, xT_lo_ready = sem("xT_full"), sem("xT_hi_ready"), sem("xT_lo_ready")
        proj_full, q_hi_ready, q_lo_ready = sem("proj_full"), sem("q_hi_ready"), sem("q_lo_ready")
        q_stored = [sem(f"q_stored{k}") for k in range(2)]
        k_lo_ready, k_stored, mask_stored = sem("k_lo_ready"), sem("k_stored"), sem("mask_stored")
        kv_copied, vT_full, v_copied = sem("kv_copied"), sem("vT_full"), sem("v_copied")
        mask_ready = sem("mask_ready")

        NP = IC + 1
        x_bank = [bank(psum, 0), bank(psum, 1)]
        proj_bank = [bank(psum, 2 + k) for k in range(4)]
        v_bank = bank(psum, 6)
        SMALL = 16 * 3
        EARLY, LATE = 1, 4
        AT_FIRST = (3, 5)

        block = ctx.enter_context(nc.Block())

        @block.sync
        def _(sp):
            def load_x(b):
                sp.dma_start(xin[:], x[bass.ds(b, 1)].rearrange("a (t p) d -> p (a t) d", p=P)).then_inc(x_loaded, 16)

            def store_q(b, ns):
                for n in ns:
                    sp.wait_ge(q_lo_ready, IC * b + n + 1)
                    for name, half in (("q_hi", q_hi), ("q_lo", q_lo)):
                        sp.dma_start(dram[name][bass.ds(b, 1), n * P:(n + 1) * P, :].rearrange("a p s -> p (a s)"),
                                     half[:, n % 2, :].bitcast(F32)).then_inc(q_stored[n % 2], 16)

            def store_k(b):
                sp.wait_ge(k_lo_ready, b + 1)
                for name, half in (("k_hi", k_hi), ("k_lo", k_lo)):
                    sp.dma_start(dram[name][bass.ds(b, 1)].rearrange("a p s -> p (a s)"), half[:].bitcast(F32)
                                 ).then_inc(k_stored, 16)

            load_x(0)
            for j in range(2):
                sp.dma_start(wq_stage[j], Wq[:, j * INNER // 2:(j + 1) * INNER // 2].rearrange("(c p) n -> p c n", p=P)
                             ).then_inc(wq_loaded[j], 16)
            sp.dma_start(wkv_stage, Wkv.rearrange("(c p) n -> p c n", p=P)).then_inc(wkv_loaded, 16)
            sp.wait_ge(xT_full, DC)
            load_x(1)
            store_q(0, range(0, AT_FIRST[1] - 2))
            sp.wait_ge(xT_full, 2 * DC)
            load_x(2)
            store_q(0, range(AT_FIRST[1] - 2, IC))
            store_k(0)
            with sp.Fori(1, B - 2) as b:
                sp.wait_ge(xT_full, DC * b + 2 * DC)
                load_x(b + 2)
                store_q(b, range(IC))
                store_k(b)
            for b in range(B - 2, B):
                store_q(b, range(IC))
                store_k(b)
            for k in range(2):
                sp.wait_ge(q_stored[k], 16 * IC * B)
            sp.wait_ge(k_stored, 16 * 2 * B)
            sp.wait_ge(mask_stored, 16)

        @block.gpsimd
        def _(pool):
            pool.dma_start(g_col[:], g_in.rearrange("(c p) -> p c", p=P), allow_slow_non_contiguous=True
                           ).then_inc(loaded, 16)
            pool.dma_start(mask_in, mask.rearrange("b (t s) -> (b t) s", s=P)).then_inc(loaded, 16)
            pool.dma_start(null_bias_sb[:], null_bias.partition_broadcast(P)).then_inc(loaded, 16)

            def reciprocal_std(b):
                pool.wait_ge(ln_moments, TB * b + TB)
                pool.tensor_tensor(out=rstd[:], in0=moments[:, :, 1], in1=eps[:], op=ALU.add).then_inc(ln_shifted, 1)
                pool.wait_ge(ln_shifted, b + 1)
                pool.tensor_tensor(out=rstd[:], in0=rstd[:], in1=pow_half[:], op=ALU.pow).then_inc(ln_rstd, 1)

            def negate_biases(i):
                at = BIAS_AT[i]
                tile = resident[:, at:at + H * CK[i]].rearrange("p (h n) -> p h n", h=H)
                pool.wait_ge(bias_loaded[i], 16 * 4)
                pool.tensor_scalar(out=tile[:, :, AHEAD:CK[i]], in0=tile[:, :, AHEAD:CK[i]], scalar1=-1.0, scalar2=1.0,
                                   op0=ALU.mult, op1=ALU.mult).then_inc(bias_ready, 1)
                pool.tensor_scalar(out=tile[:, :, 0], in0=null_bias_sb[:], scalar1=-1.0, scalar2=1.0,
                                   op0=ALU.mult, op1=ALU.mult).then_inc(bias_ready, 1)
                pool.memset(tile[:, :, 1], MASKED).then_inc(bias_ready, 1)
                pool.wait_ge(bias_ready, 4 * i + 3)
                last = tile[:, :, CK[i] - P:CK[i]]
                pool.affine_select(out=last, in_=last, compare_op=ALU.is_ge, fill=MASKED, base=0,
                                   pattern=[[0, H], [-1, P]], channel_multiplier=1).then_inc(bias_ready, 1)

            reciprocal_std(0)
            pool.wait_ge(loaded, SMALL)
            reciprocal_std(1)
            for b in range(2, B):
                reciprocal_std(b)
            for i in range(TB):
                negate_biases(i)

        @block.vector
        def _(dve):
            def normalise(b):
                measure(b)
                shift_and_scale(b)

            def measure(b):
                dve.wait_ge(x_loaded, 16 * b + 16)
                for t in range(TB):
                    dve.bn_stats(stats[:, t, :], xin[:, t, :]).then_inc(ln_stats, 1)
                for t in range(TB):
                    dve.wait_ge(ln_stats, TB * b + t + 1)
                    dve.memset(spare["dve"][:, t:t + 1], 0.0)
                    dve.bn_aggr(moments[:, t, :], stats[:, t, :]).then_inc(ln_moments, 1)

            def shift_and_scale(b):
                dve.wait_ge(ln_moments, TB * b + TB)
                dve.wait_ge(ln_rstd, b + 1)
                for t in range(TB):
                    dve.tensor_scalar(out=xin[:, t, :], in0=xin[:, t, :], scalar1=moments[:, t, 0:1],
                                      scalar2=rstd[:, t:t + 1], op0=ALU.subtract, op1=ALU.mult).then_inc(xn_ready, 1)

            def split_low(b, k, chunks):
                for c in chunks:
                    dve.wait_ge(xT_hi_ready, DC * b + c + 1)
                    dve.scalar_tensor_tensor(out=xT_lo[k][:, c, :], in0=x_bank[c % 2], scalar=g_col[:, c:c + 1],
                                             in1=xT_hi[k][:, c, :].bitcast(F32), op0=ALU.mult, op1=ALU.subtract
                                             ).then_inc(xT_lo_ready, 1)

            def lower_q(b, ns):
                for n in ns:
                    dve.wait_ge(q_hi_ready, IC * b + n + 1)
                    dve.scalar_tensor_tensor(out=q_lo[:, n % 2, :], in0=proj_bank[n % 4], scalar=-float(DH) ** -0.5,
                                             in1=q_hi[:, n % 2, :].bitcast(F32), op0=ALU.mult, op1=ALU.subtract
                                             ).then_inc(q_lo_ready, 1)

            def lower_k(b):
                dve.wait_ge(kv_copied, 2 * b + 2)
                dve.tensor_tensor(out=k_lo[:], in0=kv_out[0:DH, :], in1=k_hi[:].bitcast(F32), op=ALU.subtract
                                  ).then_inc(k_lo_ready, 1)

            def copy_v(b):
                dve.wait_ge(vT_full, b + 1)
                dve.tensor_copy(values[:, bass.ds(b, 1), :, :].rearrange("p a t d -> p (a t) d"),
                                v_bank.rearrange("p (t n) -> p t n", t=TB)[:, :, DH:2 * DH]).then_inc(v_copied, 1)

            def step(b, k, before=True, split=True, norm=True):
                if split:
                    split_low(b + 1, 1 - k, range(0, 2))
                if before:
                    copy_v(b - 1)
                lower_q(b, range(0, EARLY))
                if split:
                    split_low(b + 1, 1 - k, range(2, DC))
                lower_q(b, range(EARLY, LATE))
                if norm:
                    measure(b + 2)
                lower_q(b, range(LATE, LATE + 1))
                if norm:
                    shift_and_scale(b + 2)
                lower_q(b, range(LATE + 1, IC))
                lower_k(b)

            def lower_wq(j):
                part = slice(j * INNER // 2, (j + 1) * INNER // 2)
                dve.wait_ge(weights_hi, j + 1)
                dve.tensor_tensor(out=wq_lo[:, :, part], in0=wq_stage[j], in1=wq_hi[:, :, part].bitcast(F32),
                                  op=ALU.subtract).then_inc(weights_lo, 1)

            normalise(0)
            lower_wq(0)
            dve.wait_ge(loaded, SMALL)
            dve.tensor_scalar(out=mask_out[:], in0=mask_in, scalar1=-MASKED, scalar2=MASKED, op0=ALU.mult,
                              op1=ALU.add).then_inc(mask_ready, 1)
            split_low(0, 0, range(DC))
            lower_wq(1)
            dve.wait_ge(weights_hi, 3)
            dve.tensor_tensor(out=wkv_lo[:], in0=wkv_stage, in1=wkv_hi[:].bitcast(F32), op=ALU.subtract
                              ).then_inc(weights_lo, 1)
            measure(1)
            lower_q(0, range(0, 2))
            shift_and_scale(1)
            lower_q(0, range(2, AT_FIRST[0]))
            split_low(1, 1, range(0, 2))
            lower_q(0, range(AT_FIRST[0], AT_FIRST[1]))
            split_low(1, 1, range(2, DC))
            lower_q(0, range(AT_FIRST[1], AT_FIRST[1] + 1))
            measure(2)
            lower_q(0, range(AT_FIRST[1] + 1, IC - 1))
            shift_and_scale(2)
            lower_q(0, range(IC - 1, IC))
            lower_k(0)
            with dve.Fori(0, (B - 4) // 2) as g:
                step(2 * g + 1, 1)
                step(2 * g + 2, 0)
            step(B - 3, 1)
            step(B - 2, 0, norm=False)
            step(B - 1, 1, split=False, norm=False)
            copy_v(B - 1)

        @block.scalar
        def _(act):
            def split_high(b, k, chunks):
                if not (isinstance(b, int) and b == 0):
                    act.wait_ge(proj_full, NP * b - NP)
                for c in chunks:
                    act.wait_ge(xT_full, DC * b + c + 1)
                    act.activation(xT_hi[k][:, c, :], x_bank[c % 2], ACT.Copy, scale=g_col[:, c:c + 1]
                                   ).then_inc(xT_hi_ready, 1)

            def load_biases(i, g):
                tile = resident[:, BIAS_AT[i]:BIAS_AT[i] + H * CK[i]].rearrange("p (h n) -> p h n", h=H)
                act.dma_start(tile[:, bass.ds(H // 4 * g, H // 4), AHEAD:CK[i]],
                              fside[bass.ds(H // 4 * g, H // 4), i * P:(i + 1) * P, 0:CK[i] - AHEAD].rearrange("h p n -> p h n")
                              ).then_inc(bias_loaded[i], 16)

            def copy_q(b, k, biases=None):
                first = isinstance(b, int) and b == 0
                for n in range(IC):
                    if first and n == 3:
                        act.wait_ge(x_loaded, 32)
                        for i in range(TB):
                            load_biases(i, 0)
                    if biases is not None and n % 4 == 3:
                        load_biases(2 * (1 - k) + n // 4, biases)
                    if n in (AT_FIRST if first else (0, EARLY)) and not (isinstance(b, int) and b + 1 >= B):
                        split_high(b + 1, 1 - k, range(0, 2) if n == (AT_FIRST[0] if first else 0) else range(2, DC))
                    act.wait_ge(proj_full, NP * b + n + 1)
                    act.wait_ge(q_stored[n % 2], 32 * (IC // 2 * b + n // 2))
                    act.activation(q_hi[:, n % 2, :], proj_bank[n % 4], ACT.Copy, scale=-float(DH) ** -0.5
                                   ).then_inc(q_hi_ready, 1)
                act.wait_ge(proj_full, NP * b + NP)
                act.wait_ge(vT_full, b)
                act.wait_ge(k_lo_ready, b)
                act.activation(kv_out[:], proj_bank[IC % 4], ACT.Copy).then_inc(kv_copied, 1)
                act.wait_ge(k_stored, 32 * b)
                act.activation(k_hi[:], proj_bank[IC % 4][0:DH, :], ACT.Copy).then_inc(kv_copied, 1)

            for j in range(2):
                act.wait_ge(wq_loaded[j], 16)
                act.activation(wq_hi[:, :, j * INNER // 2:(j + 1) * INNER // 2], wq_stage[j], ACT.Copy
                               ).then_inc(weights_hi, 1)
                if j == 0:
                    act.wait_ge(loaded, SMALL)
                    split_high(0, 0, range(DC))
            act.wait_ge(wkv_loaded, 16)
            act.activation(wkv_hi[:], wkv_stage, ACT.Copy).then_inc(weights_hi, 1)
            act.wait_ge(mask_ready, 1)
            act.dma_start(dram["mask"].rearrange("a (t s) -> (a t) s", s=P), mask_out[:]).then_inc(mask_stored, 16)
            copy_q(0, 0)
            with act.Fori(0, (B - 2) // 2) as g:
                copy_q(2 * g + 1, 1, g + 1)
                copy_q(2 * g + 2, 0, g + 1)
            copy_q(B - 1, 1)

        @block.tensor
        def _(pe):
            def transpose_x(b, chunks):
                pe.wait_ge(xn_ready, TB * b + TB)
                for c in chunks:
                    if not (isinstance(b, int) and b == 0 and c < 2):
                        pe.wait_ge(xT_lo_ready, DC * b + c - 1)
                    for t in range(TB):
                        last = pe.transpose(x_bank[c % 2][:, t * P:(t + 1) * P], xin[:, t, c * P:(c + 1) * P], ident[:])
                    last.then_inc(xT_full, 1)

            def transpose_v(b):
                pe.wait_ge(kv_copied, 2 * b + 2)
                pe.wait_ge(v_copied, b)
                for t in range(TB):
                    last = pe.transpose(v_bank[:, t * P:(t + 1) * P], kv_out[:, t * P:(t + 1) * P], ident[:])
                last.then_inc(vT_full, 1)

            def project(b, k):
                first, has_next = isinstance(b, int) and b == 0, not (isinstance(b, int) and b + 1 >= B)
                if has_next and not first:
                    transpose_x(b + 1, range(0, 2))
                if not (isinstance(b, int) and b == 0):
                    transpose_v(b - 1)
                pe.wait_ge(xT_lo_ready, DC * b + DC)
                for n in range(NP):
                    if first and n in (0, IC // 2, IC):
                        pe.wait_ge(weights_lo, (0, IC // 2, IC).index(n) + 1)
                    if first and n == AT_FIRST[0]:
                        transpose_x(b + 1, range(0, 2))
                    if n == (AT_FIRST[1] if first else EARLY) and has_next:
                        transpose_x(b + 1, range(2, DC))
                    if n == 0:
                        pe.wait_ge(kv_copied, 2 * b)
                    elif n < 4:
                        pe.wait_ge(q_lo_ready, IC * b)
                    else:
                        pe.wait_ge(q_lo_ready, IC * b + n - 3)
                    if n < IC:
                        hi, lo = wq_hi[:, :, n * P:(n + 1) * P], wq_lo[:, :, n * P:(n + 1) * P]
                    else:
                        hi, lo = wkv_hi[:], wkv_lo[:]
                    out = proj_bank[n % 4]
                    for c in range(DC):
                        pe.matmul(out, hi[:, c, :], xT_hi[k][:, c, :], start=(c == 0), stop=False)
                        pe.matmul(out, hi[:, c, :], xT_lo[k][:, c, :], start=False, stop=False)
                        last = pe.matmul(out, lo[:, c, :], xT_hi[k][:, c, :], start=False, stop=(c == DC - 1))
                    last.then_inc(proj_full, 1)

            transpose_x(0, range(DC))
            for b in range(3):
                project(b, b % 2)
            with pe.Fori(1, (B - 2) // 2) as g:
                for i in range(2):
                    project(2 * g + 1 + i, 1 - i)
            project(B - 1, 1)
            transpose_v(B - 1)


def stage_attend(nc, cond, w_gate, w_up, w_down, dram, psum, resident, ident, spare, values, Wo, wo_stage,
                 wo_loaded):
    with ExitStack() as ctx:
        def sb(name, shape, dt=F32):
            return ctx.enter_context(nc.sbuf_tensor(name, shape, dt))

        def sem(name):
            return ctx.enter_context(nc.semaphore(name))

        queries = [sb(f"queries{i}", [P, H, P], F32R) for i in range(2)]
        queries1 = [sb(f"queries_and_ones{i}", [P, H, P], F32R) for i in range(2)]
        keys = sb("keys", [P, 2, AHEAD + S], F32R)
        keys1 = sb("keys_lo_and_mask", [P, 2, AHEAD + S], F32R)
        scores = [sb(f"scores{i}", [P, AHEAD + S]) for i in range(2)]
        null_key = sb("null_key", [P, 1])
        lowest = sb("lowest", [P, 4])
        probs = [sb(f"probs{i}", [P, HALF, AHEAD + S]) for i in range(2)]
        probsT = [sb(f"probsT{i}", [P, S]) for i in range(2)]
        sums, rsums = sb("sums", [P, 2, HALF]), sb("rsums", [P, 2, HALF])
        null_weight, null_out = sb("null_weight", [P, HALF]), sb("null_out", [P, HALF, DH])
        null_value = sb("null_value", [P, DH])
        o_out = [sb(f"o_out{i}", [P, HALF, DH]) for i in range(2)]
        w_in = [sb(f"w_in{i}", [P, D]) for i in range(2)]
        w_hi, w_lo = [sb(f"w_hi{i}", [P, D], F32R) for i in range(2)], [sb(f"w_lo{i}", [P, D], F32R) for i in range(2)]

        w_loaded, w_stored = [sem(f"w_loaded{i}") for i in range(2)], [sem(f"w_stored{i}") for i in range(2)]
        w_hi_ready, w_lo_ready = sem("w_hi_ready"), sem("w_lo_ready")
        queries_loaded = [sem(f"queries_loaded{i}") for i in range(2)]
        keys_loaded = sem("keys_loaded")
        null_loaded, null_split = sem("null_loaded"), sem("null_split")
        ones_set, keys_cleared = sem("ones_set"), sem("keys_cleared")
        scores_full, scores_biased = sem("scores_full"), sem("scores_biased")
        probs_ready, probsT_full = sem("probs_ready"), sem("probsT_full")
        probsT_even, probsT_odd = sem("probsT_even"), sem("probsT_odd")
        heads_summed, rsums_ready = sem("heads_summed"), sem("rsums_ready")
        o_scaled = [sem(f"o_scaled{i}") for i in range(2)]
        null_weighted = [sem(f"null_weighted{i}") for i in range(2)]
        null_spread, o_ready = sem("null_spread"), sem("o_ready")
        o_stored = [sem(f"o_stored{i}") for i in range(2)]

        CUT = AHEAD + 2 * P
        UB = TB * H
        HB = UB // HALF
        WC = DC + MC
        LOADS = [(2, 2, 1)[k // 2] * 16 for k in range(WC)]
        PASSES = [(queries, keys[:].rearrange("p b n -> p (b n)")), (queries1, keys1[:].rearrange("p b n -> p (b n)"))]

        def score_psum(i, u):
            start = 2 * BANK * (u % 2) + (BANK - CUT if CK[i] > BANK else 0)
            return psum[:, start:start + CK[i]]

        probsT_bank = [bank(psum, 4), bank(psum, 5)]
        o_bank = [bank(psum, 6), bank(psum, 7)]

        block = ctx.enter_context(nc.Block())

        @block.sync
        def _(sp):
            def load_queries(b, i):
                for dst, name in ((queries[i % 2][0:DH], "q_hi"), (queries[i % 2][DH:P], "q_lo"),
                                  (queries1[i % 2][0:DH], "q_hi")):
                    sp.dma_start(dst.bitcast(F32), dram[name][bass.ds(b, 1), :, i * P:(i + 1) * P].rearrange(
                        "a (h d) p -> d (a h) p", d=DH)).then_inc(queries_loaded[i % 2], 16)

            def load_keys(b):
                for dst, name in ((keys[0:DH], "k_hi"), (keys[DH:P], "k_hi"), (keys1[0:DH], "k_lo")):
                    sp.dma_start(dst[:, bass.ds(b % 2, 1), AHEAD:AHEAD + S].rearrange("p a s -> p (a s)").bitcast(F32),
                                 dram[name][bass.ds(b, 1)].rearrange("a p s -> p (a s)")).then_inc(keys_loaded, 16)
                sp.dma_start(keys1[DH:DH + 1, bass.ds(b % 2, 1), AHEAD:AHEAD + S].rearrange("p a s -> p (a s)").bitcast(F32),
                             dram["mask"][:, bass.ds(b * S, S)]
                             ).then_inc(keys_loaded, 16)

            def load_weights(e, k):
                if k < DC:
                    for n, w in enumerate((w_gate, w_up)):
                        sp.dma_start(w_in[k % 2][:, n * M:(n + 1) * M],
                                     w[bass.ds(e, 1), k * P:(k + 1) * P, :].rearrange("a p m -> p (a m)")
                                     ).then_inc(w_loaded[k % 2], 16)
                else:
                    sp.dma_start(w_in[k % 2][:], w_down[bass.ds(e, 1), (k - DC) * P:(k - DC + 1) * P, :].rearrange(
                        "a p n -> p (a n)")).then_inc(w_loaded[k % 2], 16)

            def store_weights(e, k):
                sp.wait_ge(w_lo_ready, WC * e + k + 1)
                for name, half in (("w_hi", w_hi), ("w_lo", w_lo)):
                    sp.dma_start(dram[name][bass.ds(e, 1), :, k * D:(k + 1) * D].rearrange("a p n -> p (a n)"),
                                 half[k % 2][:].bitcast(F32)).then_inc(w_stored[k % 2], 16)

            def body(b, last):
                for k in range(HB):
                    if k < WC:
                        store_weights(b, k)
                        if k + 2 < WC:
                            load_weights(b, k + 2)
                        elif not last:
                            load_weights(b + 1, k + 2 - WC)
                    if k % 2 == 0 and (k < TB or not last):
                        sp.wait_ge(scores_full, UB * b + H * (k // 2 + 1))
                        if k < TB:
                            load_queries(b, 2 + k // 2)
                        else:
                            if k == TB:
                                load_keys(b + 1)
                            load_queries(b + 1, k // 2 - 2)
                    sp.wait_ge(o_ready, HB * b + k + 1)
                    sp.dma_start(dram["o"][bass.ds(b * S + k // 2 * P, P), k % 2 * HALF * DH:(k % 2 + 1) * HALF * DH],
                                 o_out[k % 2][:].rearrange("p h d -> p (h d)")).then_inc(o_stored[k % 2], 16)

            sp.dma_start(null_value[:], cond[1:2, :].rearrange("a d -> (a d)").partition_broadcast(P)
                         ).then_inc(null_loaded, 16)
            for part in (slice(0, DH), slice(DH, P)):
                sp.dma_start(null_key[part, :], cond[0:1, :].rearrange("a d -> d a"), allow_slow_non_contiguous=True
                             ).then_inc(null_loaded, 16)
            sp.wait_ge(keys_cleared, 3)
            load_keys(0)
            load_queries(0, 0)
            load_queries(0, 1)
            load_weights(0, 0)
            load_weights(0, 1)
            sp.dma_start(wo_stage[0], Wo[0:(IC - 1) * P, :].rearrange("(c p) n -> p c n", p=P)).then_inc(wo_loaded, 16)
            sp.dma_start(wo_stage[1], Wo[(IC - 1) * P:INNER, :].rearrange("(c p) n -> p c n", p=P)
                         ).then_inc(wo_loaded, 16)
            with sp.Fori(0, B - 1) as b:
                body(b, False)
            body(B - 1, True)
            for k in range(2):
                sp.wait_ge(o_stored[k], 16 * B * HB // 2)
                sp.wait_ge(w_stored[k], 16 * B * WC)

        @block.gpsimd
        def _(pool):
            def split_weights(e, k):
                pool.wait_ge(w_loaded[k % 2], sum(LOADS[k % 2::2]) * e + sum(LOADS[k % 2:k + 1:2]))
                pool.wait_ge(w_stored[k % 2], 16 * WC * e + 32 * (k // 2))
                pool.tensor_tensor(out=spare["pool"][:, k % 2:k % 2 + 1], in0=ident[0:1, 0:1], in1=ident[0:1, 0:1],
                                   op=ALU.mult)
                pool.tensor_copy(w_hi[k % 2][:], w_in[k % 2][:]).then_inc(w_hi_ready, 1)
                pool.wait_ge(w_hi_ready, WC * e + k + 1)
                pool.tensor_tensor(out=w_lo[k % 2][:], in0=w_in[k % 2][:], in1=w_hi[k % 2][:].bitcast(F32),
                                   op=ALU.subtract).then_inc(w_lo_ready, 1)

            def body(b):
                for k in range(HB):
                    if k < WC:
                        split_weights(b, k)
                    pool.wait_ge(o_scaled[k % 2], HB // 2 * b + k // 2 + 1)
                    pool.tensor_tensor(out=null_weight[:], in0=probs[k % 2][:, :, 0], in1=rsums[:, k % 2, :],
                                       op=ALU.mult).then_inc(null_weighted[k % 2], 1)
                    pool.wait_ge(null_weighted[k % 2], HB // 2 * b + k // 2 + 1)
                    pool.tensor_tensor(out=null_out[:], in0=null_weight[:].unsqueeze(2).to_broadcast([P, HALF, DH]),
                                       in1=null_value[:].unsqueeze(1).to_broadcast([P, HALF, DH]),
                                       op=ALU.mult).then_inc(null_spread, 1)
                    pool.wait_ge(null_spread, HB * b + k + 1)
                    pool.tensor_tensor(out=o_out[k % 2][:], in0=o_out[k % 2][:], in1=null_out[:],
                                       op=ALU.add).then_inc(o_ready, 1)
                    pool.wait_ge(o_ready, HB * b + k + 1)

            pool.wait_ge(null_loaded, 48)
            body(0)
            with pool.Fori(1, B) as b:
                body(b)

        @block.vector
        def _(dve):
            def add_bias(b, n):
                i, h = n // H, n % H
                dve.wait_ge(scores_full, UB * b + n + 1)
                if not (isinstance(b, int) and b == 0 and n < 2):
                    dve.wait_ge(probs_ready, UB * b + n - 1)
                dve.memset(spare["dve"][:, n % 2:n % 2 + 1], 0.0)
                dve.tensor_tensor_reduce(out=scores[n % 2][:, 0:CK[i]], in0=score_psum(i, n), in1=bias_of(resident, i, h),
                                         scale=1.0, scalar=3.0e38, op0=ALU.add, op1=ALU.min,
                                         accum_out=lowest[:, n % 4:n % 4 + 1]).then_inc(scores_biased, 1)

            def copy_probs(b, n):
                dve.wait_ge(probsT_full, UB * b + n + 1)
                dve.tensor_copy(probsT[n % 2][:, 0:CK[n // H] - AHEAD], probsT_bank[n % 2][:, 0:CK[n // H] - AHEAD]
                                ).then_inc(probsT_odd, 1)

            def scale_half(b, k):
                dve.wait_ge(heads_summed, HB * b + k + 1)
                dve.reciprocal(rsums[:, k % 2, :], sums[:, k % 2, :]).then_inc(rsums_ready, 1)
                dve.wait_ge(rsums_ready, HB * b + k + 1)
                dve.wait_ge(o_stored[k % 2], 16 * (HB // 2 * b + k // 2))
                dve.tensor_tensor(out=o_out[k % 2][:], in0=o_bank[k % 2].rearrange("p (h d) -> p h d", d=DH),
                                  in1=rsums[:, k % 2, :].unsqueeze(2).to_broadcast([P, HALF, DH]),
                                  op=ALU.mult).then_inc(o_scaled[k % 2], 1)

            def body(b, first=False, last=False):
                for n in range(UB):
                    if n + 2 < UB:
                        add_bias(b, n + 2)
                    elif not last:
                        add_bias(b + 1, n + 2 - UB)
                    if n % 2:
                        copy_probs(b, n)
                    if n % HALF == 2:
                        if n > HALF:
                            scale_half(b, n // HALF - 1)
                        elif not first:
                            scale_half(b - 1, HB - 1)

            dve.memset(keys[:, :, 0:AHEAD].bitcast(F32), 0.0).then_inc(keys_cleared, 1)
            dve.memset(keys1[0:DH, :, 0:AHEAD].bitcast(F32), 0.0).then_inc(keys_cleared, 1)
            dve.memset(keys1[DH:P, :, :].bitcast(F32), 0.0).then_inc(keys_cleared, 1)
            for i in range(2):
                dve.memset(queries1[i][DH:P, :, :].bitcast(F32), 1.0).then_inc(ones_set, 1)
            dve.wait_ge(null_loaded, 48)
            dve.wait_ge(keys_cleared, 2)
            dve.tensor_copy(keys[:, :, 0], null_key[:].to_broadcast([P, 2])).then_inc(null_split, 1)
            dve.wait_ge(null_split, 1)
            dve.tensor_tensor(out=keys1[0:DH, :, 0], in0=null_key[0:DH, :].to_broadcast([DH, 2]),
                              in1=keys[0:DH, :, 0].bitcast(F32), op=ALU.subtract).then_inc(null_split, 1)
            add_bias(0, 0)
            add_bias(0, 1)
            body(0, first=True)
            with dve.Fori(1, B - 1) as b:
                body(b)
            body(B - 1, last=True)
            scale_half(B - 1, HB - 1)

        @block.scalar
        def _(act):
            def exponential(b, n):
                i, h, k = n // H, n % H, n // HALF
                act.wait_ge(scores_biased, UB * b + n + 1)
                if h % HALF == 0:
                    act.wait_ge(null_weighted[k % 2], HB // 2 * b + k // 2)
                act.activation(probs[k % 2][:, h % HALF, 0:CK[i]], scores[n % 2][:, 0:CK[i]], ACT.Exp,
                               bias=lowest[:, n % 4:n % 4 + 1], scale=-1.0,
                               accum_out=sums[:, k % 2, h % HALF:h % HALF + 1]).then_inc(probs_ready, 1)

            def copy_probs(b, n):
                act.wait_ge(probsT_full, UB * b + n + 1)
                act.activation(probsT[n % 2][:, 0:CK[n // H] - AHEAD], probsT_bank[n % 2][:, 0:CK[n // H] - AHEAD], ACT.Copy
                               ).then_inc(probsT_even, 1)

            def body(b, last=False):
                for n in range(UB):
                    if n % 2 == 0:
                        copy_probs(b, n)
                    if n + 2 < UB:
                        exponential(b, n + 2)
                    elif not last:
                        exponential(b + 1, n + 2 - UB)

            exponential(0, 0)
            exponential(0, 1)
            body(0)
            with act.Fori(1, B - 1) as b:
                body(b)
            body(B - 1, last=True)

        @block.tensor
        def _(pe):
            def score(b, n):
                i, h = n // H, n % H
                if n == 0:
                    pe.wait_ge(keys_loaded, 64 * b + 64)
                if h == 0:
                    pe.wait_ge(queries_loaded[i % 2], 48 * (2 * b + i // 2 + 1))
                if not (isinstance(b, int) and b == 0 and n < 2):
                    pe.wait_ge(scores_biased, UB * b + n - 1)
                whole = score_psum(i, n)
                parts = [(0, CUT), (CUT, CK[i])] if CK[i] > BANK else [(0, CK[i])]
                for lo, hi in parts:
                    for p, (qs, ks) in enumerate(PASSES):
                        last = pe.matmul(whole[:, lo:hi], qs[i % 2][:, h, :],
                                         ks[:, bass.ds((b % 2) * (AHEAD + S) + lo, hi - lo)], start=(p == 0), stop=(p == 1))
                last.then_inc(scores_full, 1)

            def transpose_probs(b, n):
                i, h, k = n // H, n % H, n // HALF
                pe.wait_ge(probs_ready, UB * b + n + 1)
                pe.wait_ge(probsT_odd if n % 2 else probsT_even, UB // 2 * b + n // 2)
                for j in range(i + 1):
                    last = pe.transpose(probsT_bank[n % 2][:, j * P:(j + 1) * P],
                                        probs[k % 2][:, h % HALF, AHEAD + j * P:AHEAD + (j + 1) * P], ident[:])
                last.then_inc(probsT_full, 1)

            def weigh_values(b, n):
                i, h, k = n // H, n % H, n // HALF
                pe.wait_ge(probsT_odd if n % 2 else probsT_even, UB // 2 * b + n // 2 + 1)
                if h % HALF == 0:
                    pe.wait_ge(o_scaled[k % 2], HB // 2 * b + k // 2)
                for j in range(i + 1):
                    last = pe.matmul(o_bank[k % 2][:, h % HALF * DH:(h % HALF + 1) * DH],
                                     probsT[n % 2][:, j * P:(j + 1) * P],
                                     values[:, bass.ds(b, 1), j, :].rearrange("p a d -> p (a d)"),
                                     start=(j == 0), stop=(j == i))
                if h % HALF == HALF - 1:
                    last.then_inc(heads_summed, 1)

            def body(b, first=False, last=False):
                for n in range(UB):
                    transpose_probs(b, n)
                    if n:
                        weigh_values(b, n - 1)
                    elif not first:
                        weigh_values(b - 1, UB - 1)
                    if n + 3 < UB:
                        score(b, n + 3)
                    elif not last:
                        score(b + 1, n + 3 - UB)

            pe.wait_ge(ones_set, 2)
            pe.wait_ge(null_split, 2)
            for n in range(3):
                score(0, n)
            body(0, first=True)
            with pe.Fori(1, B - 1) as b:
                body(b)
            body(B - 1, last=True)
            weigh_values(B - 1, UB - 1)



def stage_output(nc, x, cond, wo_stage, wo_loaded, g_out, wt, wg, dram, psum, ident, pow_half, eps, spare, logits):
    with ExitStack() as ctx:
        def sb(name, shape, dt=F32):
            return ctx.enter_context(nc.sbuf_tensor(name, shape, dt))

        def sem(name):
            return ctx.enter_context(nc.semaphore(name))

        wo_hi, wo_lo = sb("wo_hi", [P, IC, D], F32R), sb("wo_lo", [P, IC, D], F32R)
        g_rows = sb("g_rows", [P, D])
        wt_T, wg_T, cond_T = sb("wt_T", [P, DC, E]), sb("wg_T", [G, E]), sb("cond_T", [G, B])
        o_in = [sb(f"o_in{i}", [P, INNER]) for i in range(2)]
        x_in = [sb(f"x_in{i}", [P, D]) for i in range(2)]
        oT_hi = [sb(f"oT_hi{i}", [P, IC, P], F32R) for i in range(2)]
        oT_lo = [sb(f"oT_lo{i}", [P, IC, P], F32R) for i in range(2)]
        group = sb("group_logits", [P, B, E])
        stats, moments, rstd = sb("stats3", [P, 6]), sb("moments3", [P, 2, 2]), sb("rstd3", [P, 2])
        x1 = [sb(f"x1_{i}", [P, D]) for i in range(2)]
        x1T = sb("x1T", [P, DC, P])

        small_loaded = sem("small3_loaded")
        wo_hi_ready, wo_lo_ready = sem("wo_hi_ready"), sem("wo_lo_ready")
        group_full, group_copied = sem("group_full"), sem("group_copied")
        o_loaded = [sem(f"o_loaded{i}") for i in range(2)]
        x_loaded = [sem(f"x_rows_loaded{i}") for i in range(2)]
        oT_full, oT_hi_ready, oT_lo_ready = sem("oT_full"), sem("oT_hi_ready"), sem("oT_lo_ready")
        out_full = sem("out_full")
        ln_stats, ln_moments, ln_shifted, ln_rstd = (sem("ln3_stats"), sem("ln3_moments"), sem("ln3_shifted"),
                                                     sem("ln3_rstd"))
        y_ready, y_scaled, x1_ready = sem("y_ready"), sem("y_scaled"), sem("x1_ready")
        x1_stored = [sem(f"x1_stored{i}") for i in range(2)]
        x1T_full, x1T_copied, logits_full, logits_copied = (sem("x1T_full"), sem("x1T_copied"), sem("logits_full"),
                                                            sem("logits_copied"))

        WO_PARTS = [(0, 4), (4, IC - 1), (IC - 1, IC)]

        WO_STARTS = [lo for lo, hi in WO_PARTS]

        def wo_part(j):
            lo, hi = WO_PARTS[j]
            return wo_stage[0][:, lo:hi, :] if hi < IC else wo_stage[1]

        x_rows = x.rearrange("b s d -> (b s) d")
        oT_bank = [[bank(psum, 2 * k + j) for j in range(2)] for k in range(2)]
        out_bank = [bank(psum, 4 + k) for k in range(2)]
        x1T_bank, logits_bank = bank(psum, 6), bank(psum, 7)
        group_out = logits_bank[:, T * E:T * E + B * E]

        def steps(eng, step):
            for t in range(2):
                step(t, t % 2, t // 2)
            with eng.Fori(1, T // 2 - 1) as m:
                for k in range(2):
                    step(2 * m + k, k, m)
            for t in range(T - 2, T):
                step(t, t % 2, t // 2)

        def known(t):
            return isinstance(t, int)

        block = ctx.enter_context(nc.Block())

        @block.sync
        def _(sp):
            def load_o(t, k):
                sp.dma_start(o_in[k][:], dram["o"][bass.ds(t * P, P), :]).then_inc(o_loaded[k], 16)

            def load_x(t, k):
                sp.dma_start(x_in[k][:], x_rows[bass.ds(t * P, P), :]).then_inc(x_loaded[k], 16)

            def store_x1(t, k):
                sp.wait_ge(x1_ready, t + 1)
                sp.dma_start(dram["x1"][bass.ds(t * P, P), :], x1[k][:]).then_inc(x1_stored[k], 16)

            def step(t, k, m):
                if not (known(t) and t + 2 >= T):
                    sp.wait_ge(oT_full, 2 * t + 2)
                    load_o(t + 2, k)
                if not (known(t) and t == 0):
                    store_x1(t - 1, 1 - k)
                if not (known(t) and t + 1 >= T):
                    load_x(t + 1, 1 - k)

            load_o(0, 0)
            load_o(1, 1)
            load_x(0, 0)
            steps(sp, step)
            store_x1(T - 1, 1)
            for k in range(2):
                sp.wait_ge(x1_stored[k], 16 * T // 2)

        @block.gpsimd
        def _(pool):
            pool.dma_start(g_rows[:], g_out.partition_broadcast(P)).then_inc(small_loaded, 16)
            with nc.allow_non_contiguous_dma(reason="small weights, transposed as they come"):
                pool.dma_start(wg_T[:], wg.rearrange("e g -> g e")).then_inc(small_loaded, 16)
                pool.dma_start(cond_T[:], cond.rearrange("b g -> g b")).then_inc(small_loaded, 16)
                for c in range(DC):
                    pool.dma_start(wt_T[:, c, :], wt[:, c * P:(c + 1) * P].rearrange("e p -> p e")
                                   ).then_inc(small_loaded, 16)
            pool.wait_ge(small_loaded, 16 * (3 + DC))

            def step(t, k, m):
                pool.wait_ge(ln_moments, t + 1)
                pool.tensor_tensor(out=rstd[:, k:k + 1], in0=moments[:, k, 1:2], in1=eps[:, 0:1], op=ALU.add
                                   ).then_inc(ln_shifted, 1)
                pool.wait_ge(ln_shifted, t + 1)
                pool.tensor_tensor(out=rstd[:, k:k + 1], in0=rstd[:, k:k + 1], in1=pow_half[:, 0:1], op=ALU.pow
                                   ).then_inc(ln_rstd, 1)
                pool.wait_ge(y_ready, t + 1)
                pool.tensor_tensor(out=x1[k][:], in0=x1[k][:], in1=g_rows[:], op=ALU.mult).then_inc(y_scaled, 1)
                pool.wait_ge(y_scaled, t + 1)
                pool.wait_ge(x_loaded[k], 16 * m + 16)
                pool.tensor_tensor(out=x1[k][:], in0=x1[k][:], in1=x_in[k][:], op=ALU.add).then_inc(x1_ready, 1)

            steps(pool, step)

        @block.vector
        def _(dve):
            def split_low(t, k):
                for j in range(2):
                    dve.wait_ge(oT_hi_ready, 2 * t + j + 1)
                    dve.tensor_tensor(out=oT_lo[k][:, 4 * j:4 * j + 4, :].rearrange("p c n -> p (c n)"), in0=oT_bank[k][j],
                                      in1=oT_hi[k][:, 4 * j:4 * j + 4, :].rearrange("p c n -> p (c n)").bitcast(F32),
                                      op=ALU.subtract).then_inc(oT_lo_ready, 1)

            def step(t, k, m):
                if not (known(t) and t + 1 >= T):
                    split_low(t + 1, 1 - k)
                dve.wait_ge(out_full, t + 1)
                dve.bn_stats(stats[:], out_bank[k]).then_inc(ln_stats, 1)
                dve.wait_ge(ln_stats, t + 1)
                dve.memset(spare["dve"][:, 0:1], 0.0)
                dve.bn_aggr(moments[:, k, :], stats[:]).then_inc(ln_moments, 1)
                dve.wait_ge(ln_moments, t + 1)
                dve.wait_ge(ln_rstd, t + 1)
                dve.wait_ge(x1_stored[k], 16 * m)
                if not (known(t) and t < 2):
                    dve.wait_ge(x1T_full, t - 1)
                dve.tensor_scalar(out=x1[k][:], in0=out_bank[k], scalar1=moments[:, k, 0:1], scalar2=rstd[:, k:k + 1],
                                  op0=ALU.subtract, op1=ALU.mult).then_inc(y_ready, 1)

            for j, (lo, hi) in enumerate(WO_PARTS):
                dve.wait_ge(wo_hi_ready, j + 1)
                dve.tensor_tensor(out=wo_lo[:, lo:hi, :], in0=wo_part(j), in1=wo_hi[:, lo:hi, :].bitcast(F32),
                                  op=ALU.subtract).then_inc(wo_lo_ready, 1)
            split_low(0, 0)
            steps(dve, step)
            dve.wait_ge(group_full, 1)
            dve.wait_ge(logits_full, T)
            dve.tensor_copy(group[:], group_out.rearrange("p (b e) -> p b e", e=E)).then_inc(group_copied, 1)
            dve.wait_ge(group_copied, 1)
            dve.tensor_tensor(out=logits[:].rearrange("p (b t) e -> p b t e", t=TB),
                              in0=logits_bank[:, 0:T * E].rearrange("p (b t e) -> p b t e", t=TB, e=E),
                              in1=group[:].unsqueeze(2).to_broadcast([P, B, TB, E]), op=ALU.add
                              ).then_inc(logits_copied, 1)

        @block.scalar
        def _(act):
            def split_high(t, k):
                if not (known(t) and t < 2):
                    act.wait_ge(out_full, t - 1)
                for j in range(2):
                    act.wait_ge(oT_full, 2 * t + j + 1)
                    act.activation(oT_hi[k][:, 4 * j:4 * j + 4, :].rearrange("p c n -> p (c n)"), oT_bank[k][j], ACT.Copy
                                   ).then_inc(oT_hi_ready, 1)

            def copy_x1T(t):
                act.wait_ge(x1T_full, t + 1)
                act.activation(x1T[:].rearrange("p c n -> p (c n)"), x1T_bank, ACT.Copy).then_inc(x1T_copied, 1)

            def step(t, k, m):
                if not (known(t) and t + 1 >= T):
                    split_high(t + 1, 1 - k)
                if not (known(t) and t == 0):
                    copy_x1T(t - 1)

            act.wait_ge(wo_loaded, 32)
            for j, (lo, hi) in enumerate(WO_PARTS):
                act.activation(wo_hi[:, lo:hi, :], wo_part(j), ACT.Copy).then_inc(wo_hi_ready, 1)
            split_high(0, 0)
            steps(act, step)
            copy_x1T(T - 1)

        @block.tensor
        def _(pe):
            def transpose_o(t, k, m):
                pe.wait_ge(o_loaded[k], 16 * m + 16)
                if not (known(t) and t < 2):
                    pe.wait_ge(oT_lo_ready, 2 * t - 2)
                for j in range(2):
                    for c in range(4):
                        last = pe.transpose(oT_bank[k][j][:, c * P:(c + 1) * P],
                                            o_in[k][:, (4 * j + c) * P:(4 * j + c + 1) * P], ident[:])
                    last.then_inc(oT_full, 1)

            def project(t, k):
                pe.wait_ge(oT_lo_ready, 2 * t + 2)
                if not (known(t) and t < 2):
                    pe.wait_ge(y_ready, t - 1)
                for c in range(IC):
                    if known(t) and t == 0 and c in WO_STARTS:
                        pe.wait_ge(wo_lo_ready, WO_STARTS.index(c) + 1)
                    pe.matmul(out_bank[k], oT_hi[k][:, c, :], wo_hi[:, c, :], start=(c == 0), stop=False)
                    pe.matmul(out_bank[k], oT_hi[k][:, c, :], wo_lo[:, c, :], start=False, stop=False)
                    last = pe.matmul(out_bank[k], oT_lo[k][:, c, :], wo_hi[:, c, :], start=False, stop=(c == IC - 1))
                last.then_inc(out_full, 1)

            def group_logits():
                pe.wait_ge(small_loaded, 16 * (3 + DC))
                for b in range(B):
                    last = pe.matmul(group_out[:, b * E:(b + 1) * E], cond_T[:, b:b + 1].to_broadcast([G, P]), wg_T[:],
                                     start=True, stop=True)
                last.then_inc(group_full, 1)

            def transpose_x1(t, k):
                pe.wait_ge(x1_ready, t + 1)
                pe.wait_ge(x1T_copied, t)
                for c in range(DC):
                    last = pe.transpose(x1T_bank[:, c * P:(c + 1) * P], x1[k][:, c * P:(c + 1) * P], ident[:])
                last.then_inc(x1T_full, 1)

            def route(t):
                pe.wait_ge(x1T_copied, t + 1)
                for c in range(DC):
                    last = pe.matmul(logits_bank[:, bass.ds(t * E, E)], x1T[:, c, :], wt_T[:, c, :],
                                     start=(c == 0), stop=(c == DC - 1))
                last.then_inc(logits_full, 1)

            def step(t, k, m):
                if not (known(t) and t + 1 >= T):
                    transpose_o(t + 1, 1 - k, m + k)
                if not (known(t) and t < 2):
                    route(t - 2)
                project(t, k)
                if not (known(t) and t == 0):
                    transpose_x1(t - 1, 1 - k)
                if known(t) and t == 1:
                    group_logits()

            transpose_o(0, 0, 0)
            steps(pe, step)
            route(T - 2)
            transpose_x1(T - 1, 1)
            route(T - 1)


def stage_route(nc, sw_gate, sw_up, sw_down, dram, psum, logits, shared, route, experts, experts_loaded):
    with ExitStack() as ctx:
        def sb(name, shape, dt=F32):
            return ctx.enter_context(nc.sbuf_tensor(name, shape, dt))

        def sem(name):
            return ctx.enter_context(nc.semaphore(name))

        NTE = [P, T, E]
        w_stage = [sb(f"shared_stage{i}", [P, DC, SM]) for i in range(2)]
        PAIRS = TOPK * T
        HOT = 16
        expert_no, row_no, tile_no = sb("expert_no", [P, E]), sb("row_no", [P, P]), sb("tile_no", [P, SLOT_TILES])
        filled, token_no = sb("filled_at", [P, T]), sb("token_no", [P, TOPK * T])
        before, ones = sb("before", [P, P]), sb("ones", [P, P])
        first, second, taken, both = sb("first", NTE), sb("second", NTE), sb("taken", NTE), sb("both", NTE)
        work, shifted, totals = sb("work", NTE), sb("shifted", NTE), sb("totals", NTE)
        runs = [sb(f"runs{i}", NTE) for i in range(2)]
        best, low = sb("best", [P, TOPK, T]), sb("low4", [P, T])
        exps, exp_sum, gap, score = sb("exps", NTE), sb("exp_sum", [P, T]), sb("gap", [P, T]), sb("score", [P, TOPK, T])
        norm = sb("norm", [P, T])
        more, tiles = sb("more", [P, E, T]), sb("tiles", [P, E])
        ends = [sb(f"ends{i}", [P, E]) for i in range(2)]
        ended, owner = sb("ended", [P, SLOT_TILES, E]), sb("owner", [P, SLOT_TILES])
        tile_expert, owner_past = sb("tile_expert", [1, SLOT_TILES]), sb("owner_past", [1, SLOT_TILES])
        slot_f, slot_part = sb("slot_f", [P, TOPK, T]), sb("slot_part", [P, 2, TOPK * T], I32)
        slot_tile, slot_row = sb("slot_tile", [P, TOPK * T]), sb("slot_row", [P, TOPK * T])
        row_hot = [sb(f"row_hot{i}", [P, HOT, P], F32R) for i in range(2)]
        tile_hot = [sb(f"tile_hot{i}", [P, HOT, SLOT_TILES], F32R) for i in range(2)]
        in_tile = [sb(f"in_tile{i}", [P, HOT, SLOT_TILES]) for i in range(2)]

        iotas, step, both_ready = sem("iotas"), sem("routing_step"), sem("both_ready")
        shifted_ready, exps_ready = sem("shifted_ready"), sem("exps_ready")
        counts_full, hot_used = sem("counts_full"), sem("hot_used")
        slots_split, row_hot_ready, in_tile_ready, tile_hot_ready = (sem("slots_split"), sem("row_hot_ready"),
                                                                     sem("in_tile_ready"), sem("tile_hot_ready"))
        shared_loaded = [sem(f"shared_loaded{n}") for n in range(3)]
        shared_hi_ready, shared_lo_ready = sem("shared_hi_ready"), sem("shared_lo_ready")
        pre_bank, total_bank, token_bank = bank(psum, 0), bank(psum, 1), bank(psum, 2)

        def grid(a):
            return a.rearrange("p (t e) -> p t e", e=E)

        block = ctx.enter_context(nc.Block())

        @block.sync
        def _(sp):
            for n, w in enumerate((sw_gate, sw_up, sw_down)):
                if n == 2:
                    sp.wait_ge(shared_lo_ready, 1)
                sp.dma_start(w_stage[n % 2][:], w.rearrange("(c p) n -> p c n", p=P)).then_inc(shared_loaded[n], 16)
            for e in range(PLACES):
                load_expert(sp, dram, experts, e, experts_loaded)

        @block.gpsimd
        def _(pool):
            pool.iota(expert_no[:], pattern=[[1, E]], base=0, channel_multiplier=0,
                      allow_small_or_imprecise_dtypes=True).then_inc(iotas, 1)
            pool.memset(before[:], 1.0).then_inc(iotas, 1)
            pool.memset(ones[:], 1.0).then_inc(iotas, 1)
            pool.wait_ge(iotas, 3)
            pool.affine_select(out=before[:], in_=before[:], compare_op=ALU.is_ge, fill=0.0, base=-1,
                               pattern=[[1, P]], channel_multiplier=-1).then_inc(iotas, 1)
            for out, pattern, channel in ((filled, [[P, T]], 0), (tile_no, [[1, SLOT_TILES]], 0),
                                          (row_no, [[1, P]], 0), (token_no, [[0, TOPK], [P, T]], 1)):
                pool.iota(out[:], pattern=pattern, base=0, channel_multiplier=channel,
                          allow_small_or_imprecise_dtypes=True).then_inc(iotas, 1)
            pool.wait_ge(iotas, 8)
            pool.memset(filled[:, 0:1], -1.0).then_inc(iotas, 1)
            for n in range(3):
                pool.wait_ge(shared_hi_ready, n + 1)
                pool.tensor_tensor(out=shared["lo"][n][:], in0=w_stage[n % 2][:],
                                   in1=shared["hi"][n][:].bitcast(F32), op=ALU.subtract).then_inc(shared_lo_ready, 1)
            for g in range(PAIRS // HOT):
                pool.wait_ge(in_tile_ready, g + 1)
                if g >= 2:
                    pool.wait_ge(hot_used, g - 1)
                pool.tensor_tensor(out=tile_hot[g % 2][:], in0=in_tile[g % 2][:],
                                   in1=token_no[:, HOT * g:HOT * (g + 1)].unsqueeze(2).to_broadcast([P, HOT, SLOT_TILES]),
                                   op=ALU.mult).then_inc(tile_hot_ready, 1)

        @block.scalar
        def _(act):
            def split_high(n):
                act.wait_ge(shared_loaded[n], 16)
                act.activation(shared["hi"][n][:], w_stage[n % 2][:], ACT.Copy).then_inc(shared_hi_ready, 1)

            split_high(0)
            act.wait_ge(shifted_ready, 2)
            act.activation(exps[:], shifted[:], ACT.Exp, scale=0.5).then_inc(exps_ready, 1)
            act.activation(score[:, 1, :], gap[:], ACT.Exp, scale=0.5).then_inc(exps_ready, 1)
            split_high(1)
            split_high(2)

        @block.vector
        def _(dve):
            done = [0]

            def then(instruction):
                done[0] += 1
                instruction.then_inc(step, 1)
                dve.wait_ge(step, done[0])

            def over_experts(a):
                return a.unsqueeze(2).to_broadcast(NTE)

            def over_tiles(a):
                return a.unsqueeze(1).to_broadcast(NTE)

            def pick(hot, values, n):
                then(dve.tensor_reduce(out=best[:, n, :], in_=values[:], axis=AX.X, op=ALU.max))
                then(dve.tensor_tensor(out=work[:], in0=values[:], in1=over_experts(best[:, n, :]), op=ALU.is_equal))
                then(dve.scalar_tensor_tensor(out=work[:], in0=work[:], scalar=-float(E), in1=over_tiles(expert_no[:]),
                                              op0=ALU.mult, op1=ALU.add))
                then(dve.tensor_reduce(out=low[:], in_=work[:], axis=AX.X, op=ALU.min))
                then(dve.tensor_tensor(out=hot[:], in0=work[:], in1=over_experts(low[:]), op=ALU.is_equal))

            dve.wait_ge(iotas, 1)
            pick(first, logits, 0)
            then(dve.scalar_tensor_tensor(out=taken[:], in0=first[:], scalar=-MASKED, in1=logits[:], op0=ALU.mult,
                                          op1=ALU.add))
            pick(second, taken, 1)
            dve.tensor_tensor(out=both[:], in0=first[:], in1=second[:], op=ALU.add).then_inc(both_ready, 1)
            dve.tensor_tensor(out=shifted[:], in0=logits[:], in1=over_experts(best[:, 0, :]), op=ALU.subtract
                              ).then_inc(shifted_ready, 1)
            dve.tensor_tensor(out=gap[:], in0=best[:, 1, :], in1=best[:, 0, :], op=ALU.subtract
                              ).then_inc(shifted_ready, 1)
            dve.wait_ge(iotas, 9)
            dve.wait_ge(counts_full, 1)
            dve.tensor_copy(totals[:], grid(total_bank[:, 0:T * E]))
            then(dve.tensor_copy(runs[0][:], grid(total_bank[:, 0:T * E])))
            src, far = 0, 1
            while far < T:
                dve.tensor_copy(runs[1 - src][:, 0:far, :], runs[src][:, 0:far, :]).then_inc(step, 1)
                done[0] += 1
                then(dve.tensor_tensor(out=runs[1 - src][:, far:T, :], in0=runs[src][:, far:T, :],
                                       in1=runs[src][:, 0:T - far, :], op=ALU.add))
                src, far = 1 - src, 2 * far
            then(dve.tensor_tensor(out=more[:], in0=runs[src][:, T - 1, :].unsqueeze(2).to_broadcast([P, E, T]),
                                   in1=filled[:].unsqueeze(1).to_broadcast([P, E, T]), op=ALU.is_gt))
            then(dve.tensor_reduce(out=tiles[:], in_=more[:], axis=AX.X, op=ALU.add))
            then(dve.tensor_copy(ends[0][:], tiles[:]))
            end, far = 0, 1
            while far < E:
                dve.tensor_copy(ends[1 - end][:, 0:far], ends[end][:, 0:far]).then_inc(step, 1)
                done[0] += 1
                then(dve.tensor_tensor(out=ends[1 - end][:, far:E], in0=ends[end][:, far:E], in1=ends[end][:, 0:E - far],
                                       op=ALU.add))
                end, far = 1 - end, 2 * far
            then(dve.tensor_tensor(out=ended[:], in0=ends[end][:].unsqueeze(1).to_broadcast([P, SLOT_TILES, E]),
                                   in1=tile_no[:].unsqueeze(2).to_broadcast([P, SLOT_TILES, E]), op=ALU.is_le))
            then(dve.tensor_reduce(out=owner[:], in_=ended[:], axis=AX.X, op=ALU.add))
            dve.tensor_copy(route["ends"][:], ends[end][0:1, :]).then_inc(step, 1)
            done[0] += 1
            then(dve.tensor_scalar(out=owner[:], in0=owner[:], scalar1=float(E - 1), scalar2=None, op0=ALU.min))
            then(dve.tensor_copy(tile_expert[:], owner[0:1, :]))
            for n in range(PLACES, E, PLACES):
                then(dve.tensor_scalar(out=owner_past[:], in0=tile_expert[:], scalar1=float(n), scalar2=-float(PLACES),
                                       op0=ALU.is_ge, op1=ALU.mult))
                then(dve.tensor_tensor(out=owner[0:1, :], in0=owner[0:1, :], in1=owner_past[:], op=ALU.add))
            then(dve.tensor_scalar(out=owner[0:1, :], in0=owner[0:1, :], scalar1=float(2 * EW * E), scalar2=None,
                                   op0=ALU.mult))
            then(dve.tensor_tensor(out=route["experts"][:], in0=owner[0:1, :], in1=tile_expert[:], op=ALU.add))
            then(dve.tensor_tensor(out=tiles[:], in0=ends[end][:], in1=tiles[:], op=ALU.subtract))
            then(dve.tensor_scalar(out=tiles[:], in0=tiles[:], scalar1=float(P), scalar2=None, op0=ALU.mult))
            then(dve.tensor_tensor(out=work[:], in0=runs[src][:], in1=totals[:], op=ALU.subtract))
            then(dve.tensor_tensor(out=work[:], in0=work[:], in1=over_tiles(tiles[:]), op=ALU.add))
            then(dve.tensor_tensor(out=work[:], in0=grid(pre_bank[:, 0:T * E]), in1=work[:], op=ALU.add))
            for n, hot in enumerate((first, second)):
                then(dve.tensor_tensor(out=taken[:], in0=hot[:], in1=work[:], op=ALU.mult))
                then(dve.tensor_reduce(out=slot_f[:, n, :], in_=taken[:], axis=AX.X, op=ALU.add))
            then(dve.tensor_copy(route["slots"][:], slot_f[:]))
            flat = route["slots"][:].rearrange("p k t -> p (k t)")
            dve.tensor_scalar(out=slot_part[:, 0, :], in0=flat, scalar1=7, scalar2=None, op0=ALU.arith_shift_right
                              ).then_inc(step, 1)
            done[0] += 1
            then(dve.tensor_scalar(out=slot_part[:, 1, :], in0=flat, scalar1=P - 1, scalar2=None, op0=ALU.bitwise_and))
            dve.tensor_copy(slot_tile[:], slot_part[:, 0, :]).then_inc(slots_split, 1)
            dve.tensor_copy(slot_row[:], slot_part[:, 1, :]).then_inc(slots_split, 1)
            dve.wait_ge(slots_split, 2)
            for g in range(PAIRS // HOT):
                if g >= 2:
                    dve.wait_ge(tile_hot_ready, g - 1)
                dve.tensor_tensor(out=in_tile[g % 2][:], in0=tile_no[:].unsqueeze(1).to_broadcast([P, HOT, SLOT_TILES]),
                                  in1=slot_tile[:, HOT * g:HOT * (g + 1)].unsqueeze(2).to_broadcast([P, HOT, SLOT_TILES]),
                                  op=ALU.is_equal).then_inc(in_tile_ready, 1)
                if g >= 2:
                    dve.wait_ge(hot_used, g - 1)
                dve.tensor_tensor(out=row_hot[g % 2][:], in0=row_no[:].unsqueeze(1).to_broadcast([P, HOT, P]),
                                  in1=slot_row[:, HOT * g:HOT * (g + 1)].unsqueeze(2).to_broadcast([P, HOT, P]),
                                  op=ALU.is_equal).then_inc(row_hot_ready, 1)
            dve.wait_ge(exps_ready, 2)
            then(dve.tensor_reduce(out=exp_sum[:], in_=exps[:], axis=AX.X, op=ALU.add))
            then(dve.reciprocal(score[:, 0, :], exp_sum[:]))
            then(dve.tensor_tensor(out=score[:, 1, :], in0=score[:, 1, :], in1=score[:, 0, :], op=ALU.mult))
            then(dve.tensor_tensor(out=norm[:], in0=score[:, 0, :], in1=score[:, 1, :], op=ALU.add))
            then(dve.tensor_scalar(out=norm[:], in0=norm[:], scalar1=TINY, scalar2=None, op0=ALU.add))
            then(dve.reciprocal(exp_sum[:], norm[:]))
            then(dve.tensor_tensor(out=route["weights"][:], in0=score[:],
                                   in1=exp_sum[:].unsqueeze(1).to_broadcast([P, TOPK, T]), op=ALU.mult))
            dve.wait_ge(hot_used, PAIRS // HOT)
            then(dve.tensor_copy(route["tokens"][:], token_bank[:, 0:SLOT_TILES]))

        @block.tensor
        def _(pe):
            pe.wait_ge(both_ready, 1)
            pe.wait_ge(iotas, 4)
            flat = both[:].rearrange("p t e -> p (t e)")
            pe.matmul(pre_bank[:, 0:T * E], before[:], flat, start=True, stop=True)
            pe.matmul(total_bank[:, 0:T * E], ones[:], flat, start=True, stop=True).then_inc(counts_full, 1)

            for g in range(PAIRS // HOT):
                pe.wait_ge(row_hot_ready, g + 1)
                pe.wait_ge(tile_hot_ready, g + 1)
                for n in range(HOT):
                    last = pe.matmul(token_bank[:, 0:SLOT_TILES], row_hot[g % 2][:, n, :], tile_hot[g % 2][:, n, :],
                                     start=(HOT * g + n == 0), stop=(HOT * g + n == PAIRS - 1))
                last.then_inc(hot_used, 1)


def stage_experts(nc, dram, psum, ident, spare, experts, experts_loaded, route, x1, x1_loaded):
    with ExitStack() as ctx:
        def sb(name, shape, dt=F32):
            return ctx.enter_context(nc.sbuf_tensor(name, shape, dt))

        def sem(name):
            return ctx.enter_context(nc.semaphore(name))

        rows = [sb(f"slot_rows{i}", [P, 1], I32) for i in range(2)]
        xg = [sb(f"xg{i}", [P, D]) for i in range(2)]
        xT_hi = [sb(f"xT5_hi{i}", [P, DC, P], F32R) for i in range(2)]
        xT_lo = [sb(f"xT5_lo{i}", [P, DC, P], F32R) for i in range(2)]
        leak = [sb(f"leak{i}", [P, M]) for i in range(2)]
        hidden = [sb(f"hidden{i}", [P, M]) for i in range(2)]
        hT_hi = [sb(f"hT_hi{i}", [P, MC, P], F32R) for i in range(2)]
        hT_lo = [sb(f"hT_lo{i}", [P, MC, P], F32R) for i in range(2)]
        y_out = [sb(f"y_out{i}", [P, D]) for i in range(2)]

        experts_ready, rows_ready = sem("experts_ready"), sem("rows_ready")
        xg_loaded = [sem(f"xg_loaded{i}") for i in range(2)]
        xT_full, xT_hi_ready, xT_lo_ready = sem("xT5_full"), sem("xT5_hi_ready"), sem("xT5_lo_ready")
        up_full = sem("gate_up_full")
        leak_ready, leaky_ready, hidden_ready = sem("leak_ready"), sem("leaky_ready"), sem("hidden_ready")
        hT_full, hT_hi_ready, hT_lo_ready = sem("hT_full"), sem("hT_hi_ready"), sem("hT_lo_ready")
        y_full, y_copied = sem("y_full"), sem("y_copied")
        ys_stored = [sem(f"ys_stored{i}") for i in range(2)]

        xT_bank, up_bank = [bank(psum, k) for k in (0, 1)], [bank(psum, k) for k in (2, 3)]
        hT_bank, y_bank = [bank(psum, k) for k in (4, 5)], [bank(psum, k) for k in (6, 7)]
        N = SLOT_TILES

        def steps(eng, step):
            for s in range(4):
                step(s, s % 2, s // 2)
            with eng.Fori(2, N // 2 - 1) as m:
                for k in range(2):
                    step(2 * m + k, k, m)
            step(N - 2, 0, N // 2 - 1)
            step(N - 1, 1, N // 2 - 1)

        def known(s):
            return isinstance(s, int)

        def has_next(s):
            return not (known(s) and s + 1 >= N)

        def has_last(s):
            return not (known(s) and s == 0)

        def from_third(s):
            return not (known(s) and s < 2)

        block = ctx.enter_context(nc.Block())

        @block.gpsimd
        def _(pool):
            def step(s, k, m):
                if from_third(s):
                    pool.wait_ge(xT_full, s - 1)
                pool.tensor_copy(rows[k][:], route["tokens"][:, bass.ds(s, 1)]).then_inc(rows_ready, 1)
                pool.wait_ge(rows_ready, s + 1)
                pool.tensor_tensor(out=spare["pool"][:, 0:1], in0=ident[0:1, 0:1], in1=ident[0:1, 0:1], op=ALU.mult)
                pool.indirect_dma_start(out=xg[k][:], out_offset=None, in_=dram["x1"],
                                        in_offset=bass.IndirectOffsetOnAxis(ap=rows[k][:].bitcast(U32), axis=0)
                                        ).then_inc(xg_loaded[k], 16)

            steps(pool, step)

        @block.sync
        def _(sp):
            def make_ready(e):
                sp.wait_ge(experts_loaded[e % PLACES], 32 * (e // PLACES + 1))
                sp.sem_inc(experts_ready, 1)

            make_ready(0)
            make_ready(1)
            for e in range(E - 2):
                if e + PLACES < E:
                    end = sp.value_load(route["ends"][0:1, e:e + 1], min_val=1, max_val=SLOT_TILES)
                    sp.wait_ge(y_full, end)
                    load_expert(sp, dram, experts, e + PLACES, experts_loaded)
                make_ready(e + 2)
            for b in range(2):
                load_x1(sp, dram, x1, b, b, x1_loaded)

        @block.scalar
        def _(act):
            def round_xT(s, k):
                act.wait_ge(xT_full, s + 1)
                if from_third(s):
                    act.wait_ge(up_full, s - 1)
                act.activation(xT_hi[k][:].rearrange("p c n -> p (c n)"), xT_bank[k], ACT.Copy).then_inc(xT_hi_ready, 1)

            def round_hT(s, k):
                act.wait_ge(hT_full, s + 1)
                if from_third(s):
                    act.wait_ge(y_full, s - 1)
                act.activation(hT_hi[k][:].rearrange("p c n -> p (c n)"), hT_bank[k][:, 0:M], ACT.Copy
                               ).then_inc(hT_hi_ready, 1)

            def leak_gate(s, k):
                act.wait_ge(up_full, s + 1)
                if from_third(s):
                    act.wait_ge(hidden_ready, s - 1)
                act.activation(leak[k][:], up_bank[k][:, 0:M], ACT.Copy, scale=LEAK).then_inc(leak_ready, 1)

            def store_y(s, k, m):
                act.wait_ge(y_full, s + 1)
                act.wait_ge(ys_stored[k], 16 * m)
                act.activation(y_out[k][:], y_bank[k], ACT.Copy).then_inc(y_copied, 1)
                act.wait_ge(y_copied, s + 1)
                act.dma_start(dram["ys"][bass.ds(s * P, P), :], y_out[k][:]).then_inc(ys_stored[k], 16)

            def step(s, k, m):
                if has_last(s):
                    round_hT(s - 1, 1 - k)
                if has_next(s):
                    round_xT(s + 1, 1 - k)
                leak_gate(s, k)
                if has_last(s):
                    store_y(s - 1, 1 - k, m + k - 1)

            round_xT(0, 0)
            steps(act, step)
            round_hT(N - 1, 1)
            store_y(N - 1, 1, N // 2 - 1)
            for k in range(2):
                act.wait_ge(ys_stored[k], 16 * N // 2)

        @block.vector
        def _(dve):
            def lower_xT(s, k):
                dve.wait_ge(xT_hi_ready, s + 1)
                dve.tensor_tensor(out=xT_lo[k][:].rearrange("p c n -> p (c n)"), in0=xT_bank[k],
                                  in1=xT_hi[k][:].rearrange("p c n -> p (c n)").bitcast(F32), op=ALU.subtract
                                  ).then_inc(xT_lo_ready, 1)

            def lower_hT(s, k):
                dve.wait_ge(hT_hi_ready, s + 1)
                dve.tensor_tensor(out=hT_lo[k][:].rearrange("p c n -> p (c n)"), in0=hT_bank[k][:, 0:M],
                                  in1=hT_hi[k][:].rearrange("p c n -> p (c n)").bitcast(F32), op=ALU.subtract
                                  ).then_inc(hT_lo_ready, 1)

            def step(s, k, m):
                if has_last(s):
                    lower_hT(s - 1, 1 - k)
                if has_next(s):
                    lower_xT(s + 1, 1 - k)
                dve.wait_ge(leak_ready, s + 1)
                dve.tensor_tensor(out=leak[k][:], in0=up_bank[k][:, 0:M], in1=leak[k][:], op=ALU.max
                                  ).then_inc(leaky_ready, 1)
                dve.wait_ge(leaky_ready, s + 1)
                if from_third(s):
                    dve.wait_ge(hT_full, s - 1)
                dve.tensor_tensor(out=hidden[k][:], in0=up_bank[k][:, M:2 * M], in1=leak[k][:], op=ALU.mult
                                  ).then_inc(hidden_ready, 1)

            lower_xT(0, 0)
            steps(dve, step)
            lower_hT(N - 1, 1)

        @block.tensor
        def _(pe):
            def expert_and_place(s):
                packed = pe.value_load(route["experts"][0:1, bass.ds(s, 1)], min_val=0,
                                     max_val=(PLACES - 1) * 2 * EW * E + E - 1)
                return packed % E, pe.snap(packed // E)

            def transpose_x(s, k, m):
                pe.wait_ge(xg_loaded[k], 16 * m + 16)
                if from_third(s):
                    pe.wait_ge(xT_lo_ready, s - 1)
                for c in range(DC):
                    last = pe.transpose(xT_bank[k][:, c * P:(c + 1) * P], xg[k][:, c * P:(c + 1) * P], ident[:])
                last.then_inc(xT_full, 1)

            def three(out, hi, lo, at, start, stop):
                pe.matmul(out, hi, experts[:, bass.ds(at, D)], start=start, stop=False)
                pe.matmul(out, hi, experts[:, bass.ds(at + EW, D)], start=False, stop=False)
                return pe.matmul(out, lo, experts[:, bass.ds(at, D)], start=False, stop=stop)

            def gate_up(s, k, chunks, at):
                for c in chunks:
                    last = three(up_bank[k], xT_hi[k][:, c, :], xT_lo[k][:, c, :], at + c * D, c == 0, c == DC - 1)
                return last

            def transpose_h(s, k):
                pe.wait_ge(hidden_ready, s + 1)
                if from_third(s):
                    pe.wait_ge(hT_lo_ready, s - 1)
                for c in range(MC):
                    last = pe.transpose(hT_bank[k][:, c * P:(c + 1) * P], hidden[k][:, c * P:(c + 1) * P], ident[:])
                last.then_inc(hT_full, 1)

            def down(s, k):
                at = expert_and_place(s)[1]
                pe.wait_ge(hT_lo_ready, s + 1)
                if from_third(s):
                    pe.wait_ge(y_copied, s - 1)
                for c in range(MC):
                    last = three(y_bank[k], hT_hi[k][:, c, :], hT_lo[k][:, c, :], at + (DC + c) * D, c == 0, c == MC - 1)
                last.then_inc(y_full, 1)

            def step(s, k, m):
                e, at = expert_and_place(s)
                pe.wait_ge(experts_ready, e + 1)
                pe.wait_ge(xT_lo_ready, s + 1)
                if from_third(s):
                    pe.wait_ge(hidden_ready, s - 1)
                gate_up(s, k, range(0, DC // 2), at)
                if has_last(s):
                    transpose_h(s - 1, 1 - k)
                if has_next(s):
                    transpose_x(s + 1, 1 - k, m + k)
                gate_up(s, k, range(DC // 2, DC), at).then_inc(up_full, 1)
                if has_last(s):
                    down(s - 1, 1 - k)

            transpose_x(0, 0, 0)
            steps(pe, step)
            transpose_h(N - 1, 1)
            down(N - 1, 1)


def stage_shared(nc, dram, psum, ident, spare, shared, route, x1, x1_loaded, out):
    with ExitStack() as ctx:
        def sb(name, shape, dt=F32):
            return ctx.enter_context(nc.sbuf_tensor(name, shape, dt))

        def sem(name):
            return ctx.enter_context(nc.semaphore(name))

        leak = [sb(f"leak6_{i}", [P, S])[:] for i in range(2)]
        hidden = [sb(f"hidden6_{i}", [P, S])[:] for i in range(2)]
        picked = [[sb(f"picked{i}_{j}", [P, D])[:] for j in range(TOPK)] for i in range(2)]
        total = [sb(f"total{i}", [P, D])[:] for i in range(2)]
        xT_hi = [sb(f"xT6_hi{i}", [P, DC, S], F32R) for i in range(2)]
        xT_lo = [sb(f"xT6_lo{i}", [P, DC, S], F32R) for i in range(2)]
        h_hi, h_lo = sb("h_hi", [P, SC, S], F32R), sb("h_lo", [P, SC, S], F32R)
        rows = [sb(f"picked_rows{i}", [P, TOPK], I32) for i in range(2)]

        xT_full, xT_hi_ready, xT_lo_ready = sem("xT6_full"), sem("xT6_hi_ready"), sem("xT6_lo_ready")
        up_full, leak_ready, leaky_ready, hidden_ready = (sem("up6_full"), sem("leak6_ready"), sem("leaky6_ready"),
                                                          sem("hidden6_ready"))
        h_hi_ready, h_lo_ready, y_full = sem("h_hi_ready"), sem("h_lo_ready"), sem("y6_full")
        rows_ready = sem("picked_rows_ready")
        picked_loaded = [sem(f"picked_loaded{i}") for i in range(2)]
        y_added, first_added, total_ready = sem("y_added"), sem("first_added"), sem("total_ready")
        out_stored = [sem(f"out_stored{i}") for i in range(2)]

        out_rows = out.rearrange("b s d -> (b s) d")
        xT_bank, gate_bank = [bank(psum, k) for k in (0, 1)], [bank(psum, k) for k in (2, 3)]
        up_bank, y_bank = [bank(psum, k) for k in (4, 5)], [bank(psum, k) for k in (6, 7)]
        (gate_hi, up_hi, down_hi), (gate_lo, up_lo, down_lo) = shared["hi"], shared["lo"]

        def batches(eng, step):
            step(0, 0, 0)
            step(1, 1, 0)
            with eng.Fori(1, B // 2 - 1) as m:
                for k in range(2):
                    step(2 * m + k, k, m)
            step(B - 2, 0, B // 2 - 1)
            step(B - 1, 1, B // 2 - 1)

        def known(b):
            return isinstance(b, int)

        block = ctx.enter_context(nc.Block())

        @block.sync
        def _(sp):
            def step(b, k, m):
                for t in range(TB):
                    sp.wait_ge(total_ready, TB * b + t + 1)
                    sp.dma_start(out_rows[bass.ds(b * S + t * P, P), :], total[t % 2]).then_inc(out_stored[t % 2], 16)
                if not (known(b) and b + 2 >= B):
                    load_x1(sp, dram, x1, b + 2, k, x1_loaded)

            batches(sp, step)
            for k in range(2):
                sp.wait_ge(out_stored[k], 16 * T // 2)

        @block.gpsimd
        def _(pool):
            def step(b, k, m):
                for t in range(TB):
                    n = t % 2
                    if not (known(b) and b == 0 and t < 2):
                        pool.wait_ge(total_ready, TB * b + t - 1)
                    pool.tensor_copy(rows[n][:], route["slots"][:, :, bass.ds(TB * b + t, 1)].rearrange("p k a -> p (k a)")
                                     ).then_inc(rows_ready, 1)
                    pool.wait_ge(rows_ready, TB * b + t + 1)
                    pool.tensor_tensor(out=spare["pool"][:, 0:1], in0=ident[0:1, 0:1], in1=ident[0:1, 0:1], op=ALU.mult)
                    for j in range(TOPK):
                        pool.indirect_dma_start(out=picked[n][j], out_offset=None, in_=dram["ys"],
                                                in_offset=bass.IndirectOffsetOnAxis(ap=rows[n][:, j:j + 1].bitcast(U32),
                                                                                    axis=0)
                                                ).then_inc(picked_loaded[n], 16)

            batches(pool, step)

        @block.scalar
        def _(act):
            def split_x_high(b, k):
                if not (known(b) and b < 2):
                    act.wait_ge(up_full, SC * b - SC)
                for c in range(DC):
                    act.wait_ge(xT_full, DC * b + c + 1)
                    act.activation(xT_hi[k][:, c, :], xT_bank[c % 2], ACT.Copy).then_inc(xT_hi_ready, 1)

            def step(b, k, m):
                for j in range(SC):
                    act.wait_ge(up_full, SC * b + j + 1)
                    if not (known(b) and b == 0 and j < 2):
                        act.wait_ge(h_lo_ready, SC * b + j - 1)
                    act.activation(leak[j % 2], gate_bank[j % 2], ACT.Copy, scale=LEAK).then_inc(leak_ready, 1)
                    act.wait_ge(hidden_ready, SC * b + j + 1)
                    if j == 0:
                        act.wait_ge(y_full, TB * b)
                    act.activation(h_hi[:, j, :], hidden[j % 2], ACT.Copy).then_inc(h_hi_ready, 1)
                if not (known(b) and b + 1 >= B):
                    split_x_high(b + 1, 1 - k)

            split_x_high(0, 0)
            batches(act, step)

        @block.vector
        def _(dve):
            def split_x_low(b, k, chunks):
                for c in chunks:
                    dve.wait_ge(xT_hi_ready, DC * b + c + 1)
                    dve.tensor_tensor(out=xT_lo[k][:, c, :], in0=xT_bank[c % 2], in1=xT_hi[k][:, c, :].bitcast(F32),
                                      op=ALU.subtract).then_inc(xT_lo_ready, 1)

            def step(b, k, m):
                for j in range(SC):
                    dve.wait_ge(leak_ready, SC * b + j + 1)
                    dve.tensor_tensor(out=leak[j % 2], in0=gate_bank[j % 2], in1=leak[j % 2], op=ALU.max
                                      ).then_inc(leaky_ready, 1)
                    dve.wait_ge(leaky_ready, SC * b + j + 1)
                    dve.tensor_tensor(out=hidden[j % 2], in0=up_bank[j % 2], in1=leak[j % 2], op=ALU.mult
                                      ).then_inc(hidden_ready, 1)
                    dve.wait_ge(h_hi_ready, SC * b + j + 1)
                    dve.tensor_tensor(out=h_lo[:, j, :], in0=hidden[j % 2], in1=h_hi[:, j, :].bitcast(F32),
                                      op=ALU.subtract).then_inc(h_lo_ready, 1)
                for t in range(TB):
                    if t % 2 == 0 and not (known(b) and b + 1 >= B):
                        split_x_low(b + 1, 1 - k, range(t, t + 2))
                    n = t % 2
                    done = TB * b + t + 1
                    dve.wait_ge(y_full, done)
                    dve.wait_ge(out_stored[n], 16 * (TB // 2 * b + t // 2))
                    dve.tensor_tensor(out=total[n], in0=y_bank[n], in1=x1[k][:, t, :], op=ALU.add).then_inc(y_added, 1)
                    dve.wait_ge(y_added, done)
                    dve.wait_ge(picked_loaded[n], 16 * TOPK * (TB // 2 * b + t // 2 + 1))
                    for j, added in enumerate((first_added, total_ready)):
                        dve.scalar_tensor_tensor(out=total[n], in0=picked[n][j],
                                                 scalar=route["weights"][:, j, bass.ds(TB * b + t, 1)], in1=total[n],
                                                 op0=ALU.mult, op1=ALU.add).then_inc(added, 1)
                        if j == 0:
                            dve.wait_ge(first_added, done)

            split_x_low(0, 0, range(DC))
            batches(dve, step)

        @block.tensor
        def _(pe):
            def transpose_x(b, k, m, chunks):
                pe.wait_ge(x1_loaded[k], 16 * m + 16)
                for c in chunks:
                    if not (known(b) and b == 0 and c < 2):
                        pe.wait_ge(xT_lo_ready, DC * b + c - 1)
                    for t in range(TB):
                        last = pe.transpose(xT_bank[c % 2][:, t * P:(t + 1) * P], x1[k][:, t, c * P:(c + 1) * P], ident[:])
                    last.then_inc(xT_full, 1)

            def three(out, hi, lo, rhs_hi, rhs_lo, start, stop):
                pe.matmul(out, hi, rhs_hi, start=start, stop=False)
                pe.matmul(out, hi, rhs_lo, start=False, stop=False)
                return pe.matmul(out, lo, rhs_hi, start=False, stop=stop)

            def down(t, js):
                rows = slice(t * P, (t + 1) * P)
                for j in js:
                    last = three(y_bank[t % 2], h_hi[:, j, rows], h_lo[:, j, rows], down_hi[:, j, :], down_lo[:, j, :],
                                 j == 0, j == SC - 1)
                return last

            def step(b, k, m):
                pe.wait_ge(xT_lo_ready, DC * b + DC)
                for j in range(SC):
                    if not (known(b) and b == 0 and j < 2):
                        pe.wait_ge(hidden_ready, SC * b + j - 1)
                    cols = slice(j * P, (j + 1) * P)
                    for dst, hi, lo in ((gate_bank, gate_hi, gate_lo), (up_bank, up_hi, up_lo)):
                        for c in range(DC):
                            last = three(dst[j % 2], hi[:, c, cols], lo[:, c, cols], xT_hi[k][:, c, :], xT_lo[k][:, c, :],
                                         c == 0, c == DC - 1)
                    last.then_inc(up_full, 1)
                has_next = not (known(b) and b + 1 >= B)
                if has_next:
                    transpose_x(b + 1, 1 - k, m + k, range(0, 2))
                pe.wait_ge(h_lo_ready, SC * b + SC - 1)
                for t in range(2):
                    if not (known(b) and b == 0):
                        pe.wait_ge(y_added, TB * b + t - 1)
                    down(t, range(0, SC - 1))
                pe.wait_ge(h_lo_ready, SC * b + SC)
                for t in range(2):
                    down(t, range(SC - 1, SC)).then_inc(y_full, 1)
                if has_next:
                    transpose_x(b + 1, 1 - k, m + k, range(2, DC))
                for t in range(2, TB):
                    pe.wait_ge(y_added, TB * b + t - 1)
                    down(t, range(0, SC)).then_inc(y_full, 1)

            transpose_x(0, 0, 0, range(DC))
            batches(pe, step)


_INS = ['x', 'fside_16xSxS_0', 'cond_64', 'mask_BxS_bk0', 'L0_cond_g_in', 'L0_cond_null_attn_bias', 'L0_cond_Wq',
        'L0_cond_Wkv', 'L0_cond_Wo', 'L0_cond_g_out', 'L1_cond_wt', 'L1_cond_wg', 'L1_cond_w_gate', 'L1_cond_w_up',
        'L1_cond_w_down', 'L1_cond_sw_gate', 'L1_cond_sw_up', 'L1_cond_sw_down']


def kernel(**inputs):
    import numpy as np
    import concourse.bacc as bacc
    from concourse.bass_utils import run_bass_kernel_spmd

    nc = bacc.Bacc("TRN2", target_bir_lowering=False, num_devices=1)
    arrays, args = {}, []
    for name in _INS:
        a = np.ascontiguousarray(inputs[name])
        arrays[f"in_{name}"] = a
        args.append(nc.dram_tensor(f"in_{name}", a.shape, mybir.dt.from_np(a.dtype), kind="ExternalInput").ap())
    out = nc.dram_tensor("out", (B, S, D), F32, kind="ExternalOutput").ap()
    build(nc, *args, out)
    r = run_bass_kernel_spmd(nc, [arrays], core_ids=[0])
    return r.results[0]["out"]
```
